# Optimizing a Trainium2 kernel written in Bass

```python
import numpy as np
import jax
import jax.numpy as jnp

def _softmax(x, axis=-1):
    return jax.nn.softmax(x, axis=axis)

def _gelu(x):
    return jax.nn.gelu(x, approximate=True)

def _silu(x):
    return jax.nn.silu(x)

def _sigmoid(x):
    return jax.nn.sigmoid(x)

def _layernorm(x, axis=-1, eps=1e-05):
    m = jnp.mean(x, axis=axis, keepdims=True)
    v = jnp.var(x, axis=axis, keepdims=True)
    return (x - m) / jnp.sqrt(v + eps)

def _scatter_add(tgt, idx, src, axis=0):
    return tgt.at[idx].add(src)

def _segment_sum(src, seg, n):
    return jax.ops.segment_sum(src, seg, n)
kernel_name = 'mk_early_fusion_d1_tok_img768_r4_f5163e'

def setup_inputs(seed: int=0):
    np.random.seed(seed)
    _w = jnp.asarray

    def _rec_inputs():
        import jax
        import jax.numpy as jnp
        _rk = jax.random.key(seed)
        x = 127.472 + 73.6052 * jax.random.normal(jax.random.fold_in(_rk, 1), (32, 224, 224, 3), jnp.float32)
        txt = 0.0166781 + 0.320622 * jax.random.normal(jax.random.fold_in(_rk, 2), (32, 77, 192), jnp.float32)
        return (x, txt)
    x, txt = _rec_inputs()

    def _L0_tok_setup():
        import jax, jax.numpy as jnp
        import numpy as np
        B, H, W_IMG, C = (128, 224, 224, 3)
        P = 16
        NP = H // P * (W_IMG // P)
        D = P * P * C
        PROJ = 192

        def _img2patch(images):
            b = images.shape[0]
            x = images.reshape(b, H // P, P, W_IMG // P, P, C)
            x = x.transpose(0, 1, 3, 2, 4, 5)
            return x.reshape(b, NP, D)
        key = jax.random.key(seed)
        k1, k2, k3, k4 = jax.random.split(key, 4)
        images = jax.random.uniform(k1, (B, H, W_IMG, C), dtype=jnp.float32) * 255.0
        W = jax.random.normal(k2, (D, PROJ), dtype=jnp.float32) * 0.02
        b = jnp.zeros((PROJ,), dtype=jnp.float32)
        class_token = jax.random.normal(k3, (PROJ,), dtype=jnp.float32) * 0.02
        pos_emb = jax.random.normal(k4, (NP + 1, PROJ), dtype=jnp.float32) * 0.02
        return {'images': images, 'W': W, 'b': b, 'class_token': class_token, 'pos_emb': pos_emb}
    _L0_tok_all = _L0_tok_setup()
    _L0_tok_in = {k: v for k, v in _L0_tok_all.items() if k in ('W', 'b', 'class_token', 'pos_emb')}
    del _L0_tok_all

    def _L0_attn_setup():
        import jax, jax.numpy as jnp
        import numpy as np
        D_MODEL, D_STATE, D_CONV, EXPAND = (192, 16, 4, 2)
        D_INNER = EXPAND * D_MODEL
        DT_RANK = (D_MODEL + D_STATE - 1) // D_STATE
        BATCH, L = (256, 6)

        def _mamba_params(key):
            ks = jax.random.split(key, 7)

            def w(k, shape, fan_in):
                return (jax.random.normal(k, shape) / np.sqrt(fan_in)).astype(jnp.float32)
            in_proj = w(ks[0], (2 * D_INNER, D_MODEL), D_MODEL)
            conv_w = w(ks[1], (D_CONV, D_INNER), D_CONV)
            conv_b = (jax.random.normal(ks[2], (D_INNER,)) * 0.02).astype(jnp.float32)
            x_proj = w(ks[3], (DT_RANK + 2 * D_STATE, D_INNER), D_INNER)
            dt_w = w(ks[4], (D_INNER, DT_RANK), DT_RANK)
            dt_b = (jax.random.normal(ks[5], (D_INNER,)) * 0.1).astype(jnp.float32)
            A_log = jnp.log(jnp.tile(jnp.arange(1, D_STATE + 1, dtype=jnp.float32), (D_INNER, 1)))
            Dp = jnp.ones((D_INNER,), jnp.float32)
            out_proj = w(ks[6], (D_MODEL, D_INNER), D_INNER)
            return (in_proj, conv_w, conv_b, x_proj, dt_w, dt_b, A_log, Dp, out_proj)

        def _causal_dwconv(x, conv_w, conv_b):
            Lx = x.shape[1]
            xp = jnp.pad(x, ((0, 0), (D_CONV - 1, 0), (0, 0)))
            y = sum((conv_w[k] * xp[:, k:k + Lx, :] for k in range(D_CONV)))
            return y + conv_b

        def _selective_scan(dt, Bm, Cm, u, A, Dp):

            def step(h, inp):
                dt_t, B_t, C_t, u_t = inp
                dA = jnp.exp(dt_t[..., None] * A)
                dBu = (dt_t * u_t)[..., None] * B_t[:, None, :]
                h = dA * h + dBu
                y = jnp.einsum('bdn,bn->bd', h, C_t)
                return (h, y)
            h0 = jnp.zeros((dt.shape[0], A.shape[0], A.shape[1]), dt.dtype)
            xs = (dt.swapaxes(0, 1), Bm.swapaxes(0, 1), Cm.swapaxes(0, 1), u.swapaxes(0, 1))
            _, ys = jax.lax.scan(step, h0, xs)
            return ys.swapaxes(0, 1) + u * Dp

        def _mamba(x, in_proj, conv_w, conv_b, x_proj, dt_w, dt_b, A_log, Dp, out_proj):
            xz = jnp.einsum('bld,ed->ble', x, in_proj)
            xi, z = jnp.split(xz, 2, axis=-1)
            xc = jax.nn.silu(_causal_dwconv(xi, conv_w, conv_b))
            x_dbl = jnp.einsum('bld,ed->ble', xc, x_proj)
            dt_lo, Bm, Cm = jnp.split(x_dbl, [DT_RANK, DT_RANK + D_STATE], axis=-1)
            dt = jax.nn.softplus(jnp.einsum('blr,dr->bld', dt_lo, dt_w) + dt_b)
            A = -jnp.exp(A_log)
            y = _selective_scan(dt, Bm, Cm, xc, A, Dp)
            y = y * jax.nn.silu(z)
            return jnp.einsum('bld,ed->ble', y, out_proj)

        def _forward(x, f_in, f_cw, f_cb, f_xp, f_dtw, f_dtb, f_Alog, f_D, f_out, b_in, b_cw, b_cb, b_xp, b_dtw, b_dtb, b_Alog, b_D, b_out, ln_g, ln_b):
            x_fwd = _mamba(x, f_in, f_cw, f_cb, f_xp, f_dtw, f_dtb, f_Alog, f_D, f_out)
            x_bwd = _mamba(x[:, ::-1, :], b_in, b_cw, b_cb, b_xp, b_dtw, b_dtb, b_Alog, b_D, b_out)[:, ::-1, :]
            r = x + (x_fwd + x_bwd)
            mu = jnp.mean(r, axis=-1, keepdims=True)
            var = jnp.mean(jnp.square(r - mu), axis=-1, keepdims=True)
            return (r - mu) * jax.lax.rsqrt(var + 1e-05) * ln_g + ln_b
        key = jax.random.key(seed)
        kx, kf, kb, kg = jax.random.split(key, 4)
        f = _mamba_params(kf)
        b = _mamba_params(kb)
        names_f = ['f_in', 'f_cw', 'f_cb', 'f_xp', 'f_dtw', 'f_dtb', 'f_Alog', 'f_D', 'f_out']
        names_b = ['b_in', 'b_cw', 'b_cb', 'b_xp', 'b_dtw', 'b_dtb', 'b_Alog', 'b_D', 'b_out']
        inp = {'x': jax.random.normal(kx, (BATCH, L, D_MODEL), jnp.float32)}
        inp.update(dict(zip(names_f, f)))
        inp.update(dict(zip(names_b, b)))
        inp['ln_g'] = jnp.ones((D_MODEL,), jnp.float32)
        inp['ln_b'] = jnp.zeros((D_MODEL,), jnp.float32)
        return inp
    _L0_attn_all = _L0_attn_setup()
    _L0_attn_in = {k: v for k, v in _L0_attn_all.items() if k in ('f_in', 'f_cw', 'f_cb', 'f_xp', 'f_dtw', 'f_dtb', 'f_Alog', 'f_D', 'f_out', 'b_in', 'b_cw', 'b_cb', 'b_xp', 'b_dtw', 'b_dtb', 'b_Alog', 'b_D', 'b_out', 'ln_g', 'ln_b')}
    del _L0_attn_all

    def _L0_ffn_setup():
        import jax, jax.numpy as jnp
        import numpy as np
        H = 12
        ALPHA = (1, 2, 3)
        DEPTH = 5
        BLOCK_DEPTH = 3
        TOTAL_DEPTH_M1 = 14 - 1
        SMALL_ACTIVE = BLOCK_DEPTH <= DEPTH <= TOTAL_DEPTH_M1 - BLOCK_DEPTH

        def _ln(x, g, b, eps=1e-05):
            m = jnp.mean(x, axis=-1, keepdims=True)
            v = jnp.mean((x - m) ** 2, axis=-1, keepdims=True)
            return (x - m) * jax.lax.rsqrt(v + eps) * g + b

        def _attn_branch(xp, w_qkv, w_proj, b_proj, keep_heads, keep_ch):
            B2, N, C = xp.shape
            hd = C // H
            scale = hd ** (-0.5)
            qkv = (xp @ w_qkv).reshape(B2, N, 3, H, hd).transpose(2, 0, 3, 1, 4)
            hmask = (jnp.arange(H) < keep_heads).astype(xp.dtype)[None, :, None, None]
            q, k, v = (qkv[0] * hmask, qkv[1] * hmask, qkv[2] * hmask)
            a = jax.nn.softmax(jnp.einsum('bhnd,bhmd->bhnm', q, k) * scale, axis=-1)
            o = jnp.einsum('bhnm,bhmd->bhnd', a, v).transpose(0, 2, 1, 3).reshape(B2, N, C)
            o = o @ w_proj + b_proj
            cmask = (jnp.arange(C) < keep_ch).astype(xp.dtype)
            return o * cmask

        def _mlp_branch(xp, w1, b1, w2, b2, keep_ch):
            C = xp.shape[-1]
            cmask = (jnp.arange(C) < keep_ch).astype(xp.dtype)
            h = jax.nn.gelu(xp * cmask @ w1 + b1, approximate=False)
            return (h @ w2 + b2) * cmask
        key = jax.random.key(seed)
        ks = jax.random.split(key, 8)
        B, N, C = (64, 257, 192)
        HID = 4 * C

        def w(k, shape):
            return jax.random.normal(k, shape, jnp.float32) * 0.02
        return {'x': jax.random.normal(ks[0], (B, N, C), jnp.float32), 'gumbel_weights': jax.random.uniform(ks[1], (3,), jnp.float32), 'n1l_g': jnp.ones((C,), jnp.float32), 'n1l_b': jnp.zeros((C,), jnp.float32), 'n1s_g': jnp.ones((C,), jnp.float32), 'n1s_b': jnp.zeros((C,), jnp.float32), 'w_qkv': w(ks[2], (C, 3 * C)), 'w_proj': w(ks[3], (C, C)), 'b_proj': jnp.zeros((C,), jnp.float32), 'n2l_g': jnp.ones((C,), jnp.float32), 'n2l_b': jnp.zeros((C,), jnp.float32), 'n2s_g': jnp.ones((C,), jnp.float32), 'n2s_b': jnp.zeros((C,), jnp.float32), 'w_fc1': w(ks[4], (C, HID)), 'b_fc1': jnp.zeros((HID,), jnp.float32), 'w_fc2': w(ks[5], (HID, C)), 'b_fc2': jnp.zeros((C,), jnp.float32)}
    _L0_ffn_all = _L0_ffn_setup()
    _L0_ffn_in = {k: v for k, v in _L0_ffn_all.items() if k in ('gumbel_weights', 'n1l_g', 'n1l_b', 'n1s_g', 'n1s_b', 'w_qkv', 'w_proj', 'b_proj', 'n2l_g', 'n2l_b', 'n2s_g', 'n2s_b', 'w_fc1', 'b_fc1', 'w_fc2', 'b_fc2')}
    del _L0_ffn_all
    return {'x': x, 'txt': txt, 'L0_tok_W': _L0_tok_in['W'], 'L0_tok_b': _L0_tok_in['b'], 'L0_tok_class_token': _L0_tok_in['class_token'], 'L0_tok_pos_emb': _L0_tok_in['pos_emb'], 'L0_attn_f_in': _L0_attn_in['f_in'], 'L0_attn_f_cw': _L0_attn_in['f_cw'], 'L0_attn_f_cb': _L0_attn_in['f_cb'], 'L0_attn_f_xp': _L0_attn_in['f_xp'], 'L0_attn_f_dtw': _L0_attn_in['f_dtw'], 'L0_attn_f_dtb': _L0_attn_in['f_dtb'], 'L0_attn_f_Alog': _L0_attn_in['f_Alog'], 'L0_attn_f_D': _L0_attn_in['f_D'], 'L0_attn_f_out': _L0_attn_in['f_out'], 'L0_attn_b_in': _L0_attn_in['b_in'], 'L0_attn_b_cw': _L0_attn_in['b_cw'], 'L0_attn_b_cb': _L0_attn_in['b_cb'], 'L0_attn_b_xp': _L0_attn_in['b_xp'], 'L0_attn_b_dtw': _L0_attn_in['b_dtw'], 'L0_attn_b_dtb': _L0_attn_in['b_dtb'], 'L0_attn_b_Alog': _L0_attn_in['b_Alog'], 'L0_attn_b_D': _L0_attn_in['b_D'], 'L0_attn_b_out': _L0_attn_in['b_out'], 'L0_attn_ln_g': _L0_attn_in['ln_g'], 'L0_attn_ln_b': _L0_attn_in['ln_b'], 'L0_ffn_gumbel_weights': _L0_ffn_in['gumbel_weights'], 'L0_ffn_n1l_g': _L0_ffn_in['n1l_g'], 'L0_ffn_n1l_b': _L0_ffn_in['n1l_b'], 'L0_ffn_n1s_g': _L0_ffn_in['n1s_g'], 'L0_ffn_n1s_b': _L0_ffn_in['n1s_b'], 'L0_ffn_w_qkv': _L0_ffn_in['w_qkv'], 'L0_ffn_w_proj': _L0_ffn_in['w_proj'], 'L0_ffn_b_proj': _L0_ffn_in['b_proj'], 'L0_ffn_n2l_g': _L0_ffn_in['n2l_g'], 'L0_ffn_n2l_b': _L0_ffn_in['n2l_b'], 'L0_ffn_n2s_g': _L0_ffn_in['n2s_g'], 'L0_ffn_n2s_b': _L0_ffn_in['n2s_b'], 'L0_ffn_w_fc1': _L0_ffn_in['w_fc1'], 'L0_ffn_b_fc1': _L0_ffn_in['b_fc1'], 'L0_ffn_w_fc2': _L0_ffn_in['w_fc2'], 'L0_ffn_b_fc2': _L0_ffn_in['b_fc2']}

def reference(x, txt, L0_tok_W, L0_tok_b, L0_tok_class_token, L0_tok_pos_emb, L0_attn_f_in, L0_attn_f_cw, L0_attn_f_cb, L0_attn_f_xp, L0_attn_f_dtw, L0_attn_f_dtb, L0_attn_f_Alog, L0_attn_f_D, L0_attn_f_out, L0_attn_b_in, L0_attn_b_cw, L0_attn_b_cb, L0_attn_b_xp, L0_attn_b_dtw, L0_attn_b_dtb, L0_attn_b_Alog, L0_attn_b_D, L0_attn_b_out, L0_attn_ln_g, L0_attn_ln_b, L0_ffn_gumbel_weights, L0_ffn_n1l_g, L0_ffn_n1l_b, L0_ffn_n1s_g, L0_ffn_n1s_b, L0_ffn_w_qkv, L0_ffn_w_proj, L0_ffn_b_proj, L0_ffn_n2l_g, L0_ffn_n2l_b, L0_ffn_n2s_g, L0_ffn_n2s_b, L0_ffn_w_fc1, L0_ffn_b_fc1, L0_ffn_w_fc2, L0_ffn_b_fc2):
    import jax
    import jax.numpy as jnp

    def _L0_tok_ref(images, W, b, class_token, pos_emb):
        import jax, jax.numpy as jnp
        import numpy as np
        B, H, W_IMG, C = (128, 224, 224, 3)
        P = 16
        NP = H // P * (W_IMG // P)
        D = P * P * C
        PROJ = 192

        def _img2patch(images):
            b = images.shape[0]
            x = images.reshape(b, H // P, P, W_IMG // P, P, C)
            x = x.transpose(0, 1, 3, 2, 4, 5)
            return x.reshape(b, NP, D)
        x = images / 255.0
        patches = _img2patch(x)
        proj = jnp.einsum('bnd,de->bne', patches, W) + b
        cls = jnp.broadcast_to(class_token, (images.shape[0], 1, PROJ))
        emb = jnp.concatenate([cls, proj], axis=1) + pos_emb
        return emb

    def _L0_attn_ref(x, f_in, f_cw, f_cb, f_xp, f_dtw, f_dtb, f_Alog, f_D, f_out, b_in, b_cw, b_cb, b_xp, b_dtw, b_dtb, b_Alog, b_D, b_out, ln_g, ln_b):
        import jax, jax.numpy as jnp
        import numpy as np
        D_MODEL, D_STATE, D_CONV, EXPAND = (192, 16, 4, 2)
        D_INNER = EXPAND * D_MODEL
        DT_RANK = (D_MODEL + D_STATE - 1) // D_STATE
        BATCH, L = (256, 6)

        def _mamba_params(key):
            ks = jax.random.split(key, 7)

            def w(k, shape, fan_in):
                return (jax.random.normal(k, shape) / np.sqrt(fan_in)).astype(jnp.float32)
            in_proj = w(ks[0], (2 * D_INNER, D_MODEL), D_MODEL)
            conv_w = w(ks[1], (D_CONV, D_INNER), D_CONV)
            conv_b = (jax.random.normal(ks[2], (D_INNER,)) * 0.02).astype(jnp.float32)
            x_proj = w(ks[3], (DT_RANK + 2 * D_STATE, D_INNER), D_INNER)
            dt_w = w(ks[4], (D_INNER, DT_RANK), DT_RANK)
            dt_b = (jax.random.normal(ks[5], (D_INNER,)) * 0.1).astype(jnp.float32)
            A_log = jnp.log(jnp.tile(jnp.arange(1, D_STATE + 1, dtype=jnp.float32), (D_INNER, 1)))
            Dp = jnp.ones((D_INNER,), jnp.float32)
            out_proj = w(ks[6], (D_MODEL, D_INNER), D_INNER)
            return (in_proj, conv_w, conv_b, x_proj, dt_w, dt_b, A_log, Dp, out_proj)

        def _causal_dwconv(x, conv_w, conv_b):
            Lx = x.shape[1]
            xp = jnp.pad(x, ((0, 0), (D_CONV - 1, 0), (0, 0)))
            y = sum((conv_w[k] * xp[:, k:k + Lx, :] for k in range(D_CONV)))
            return y + conv_b

        def _selective_scan(dt, Bm, Cm, u, A, Dp):

            def step(h, inp):
                dt_t, B_t, C_t, u_t = inp
                dA = jnp.exp(dt_t[..., None] * A)
                dBu = (dt_t * u_t)[..., None] * B_t[:, None, :]
                h = dA * h + dBu
                y = jnp.einsum('bdn,bn->bd', h, C_t)
                return (h, y)
            h0 = jnp.zeros((dt.shape[0], A.shape[0], A.shape[1]), dt.dtype)
            xs = (dt.swapaxes(0, 1), Bm.swapaxes(0, 1), Cm.swapaxes(0, 1), u.swapaxes(0, 1))
            _, ys = jax.lax.scan(step, h0, xs)
            return ys.swapaxes(0, 1) + u * Dp

        def _mamba(x, in_proj, conv_w, conv_b, x_proj, dt_w, dt_b, A_log, Dp, out_proj):
            xz = jnp.einsum('bld,ed->ble', x, in_proj)
            xi, z = jnp.split(xz, 2, axis=-1)
            xc = jax.nn.silu(_causal_dwconv(xi, conv_w, conv_b))
            x_dbl = jnp.einsum('bld,ed->ble', xc, x_proj)
            dt_lo, Bm, Cm = jnp.split(x_dbl, [DT_RANK, DT_RANK + D_STATE], axis=-1)
            dt = jax.nn.softplus(jnp.einsum('blr,dr->bld', dt_lo, dt_w) + dt_b)
            A = -jnp.exp(A_log)
            y = _selective_scan(dt, Bm, Cm, xc, A, Dp)
            y = y * jax.nn.silu(z)
            return jnp.einsum('bld,ed->ble', y, out_proj)

        def _forward(x, f_in, f_cw, f_cb, f_xp, f_dtw, f_dtb, f_Alog, f_D, f_out, b_in, b_cw, b_cb, b_xp, b_dtw, b_dtb, b_Alog, b_D, b_out, ln_g, ln_b):
            x_fwd = _mamba(x, f_in, f_cw, f_cb, f_xp, f_dtw, f_dtb, f_Alog, f_D, f_out)
            x_bwd = _mamba(x[:, ::-1, :], b_in, b_cw, b_cb, b_xp, b_dtw, b_dtb, b_Alog, b_D, b_out)[:, ::-1, :]
            r = x + (x_fwd + x_bwd)
            mu = jnp.mean(r, axis=-1, keepdims=True)
            var = jnp.mean(jnp.square(r - mu), axis=-1, keepdims=True)
            return (r - mu) * jax.lax.rsqrt(var + 1e-05) * ln_g + ln_b
        return _forward(x, f_in, f_cw, f_cb, f_xp, f_dtw, f_dtb, f_Alog, f_D, f_out, b_in, b_cw, b_cb, b_xp, b_dtw, b_dtb, b_Alog, b_D, b_out, ln_g, ln_b)

    def _L0_ffn_ref(x, gumbel_weights, n1l_g, n1l_b, n1s_g, n1s_b, w_qkv, w_proj, b_proj, n2l_g, n2l_b, n2s_g, n2s_b, w_fc1, b_fc1, w_fc2, b_fc2):
        import jax, jax.numpy as jnp
        import numpy as np
        H = 12
        ALPHA = (1, 2, 3)
        DEPTH = 5
        BLOCK_DEPTH = 3
        TOTAL_DEPTH_M1 = 14 - 1
        SMALL_ACTIVE = BLOCK_DEPTH <= DEPTH <= TOTAL_DEPTH_M1 - BLOCK_DEPTH

        def _ln(x, g, b, eps=1e-05):
            m = jnp.mean(x, axis=-1, keepdims=True)
            v = jnp.mean((x - m) ** 2, axis=-1, keepdims=True)
            return (x - m) * jax.lax.rsqrt(v + eps) * g + b

        def _attn_branch(xp, w_qkv, w_proj, b_proj, keep_heads, keep_ch):
            B2, N, C = xp.shape
            hd = C // H
            scale = hd ** (-0.5)
            qkv = (xp @ w_qkv).reshape(B2, N, 3, H, hd).transpose(2, 0, 3, 1, 4)
            hmask = (jnp.arange(H) < keep_heads).astype(xp.dtype)[None, :, None, None]
            q, k, v = (qkv[0] * hmask, qkv[1] * hmask, qkv[2] * hmask)
            a = jax.nn.softmax(jnp.einsum('bhnd,bhmd->bhnm', q, k) * scale, axis=-1)
            o = jnp.einsum('bhnm,bhmd->bhnd', a, v).transpose(0, 2, 1, 3).reshape(B2, N, C)
            o = o @ w_proj + b_proj
            cmask = (jnp.arange(C) < keep_ch).astype(xp.dtype)
            return o * cmask

        def _mlp_branch(xp, w1, b1, w2, b2, keep_ch):
            C = xp.shape[-1]
            cmask = (jnp.arange(C) < keep_ch).astype(xp.dtype)
            h = jax.nn.gelu(xp * cmask @ w1 + b1, approximate=False)
            return (h @ w2 + b2) * cmask
        B, N, C = x.shape
        B2 = B // 2
        nl = _ln(x[:B2], n1l_g, n1l_b)
        ns = _ln(x[B2:], n1s_g, n1s_b)
        a_large = _attn_branch(nl, w_qkv, w_proj, b_proj, H, C)
        if SMALL_ACTIVE:
            a_small = sum((gumbel_weights[i] * _attn_branch(ns, w_qkv, w_proj, b_proj, H // ALPHA[i], C // ALPHA[i]) for i in range(3)))
            attn_out = jnp.concatenate([a_large, a_small], axis=0)
        else:
            attn_out = jnp.concatenate([a_large, a_large], axis=0)
        x = x + attn_out
        nl2 = _ln(x[:B2], n2l_g, n2l_b)
        ns2 = _ln(x[B2:], n2s_g, n2s_b)
        m_large = _mlp_branch(nl2, w_fc1, b_fc1, w_fc2, b_fc2, C)
        if SMALL_ACTIVE:
            m_small = sum((gumbel_weights[i] * _mlp_branch(ns2, w_fc1, b_fc1, w_fc2, b_fc2, C // ALPHA[i]) for i in range(3)))
            mlp_out = jnp.concatenate([m_large, m_small], axis=0)
        else:
            mlp_out = jnp.concatenate([m_large, m_large], axis=0)
        return x + mlp_out
    h = _L0_tok_ref(x, L0_tok_W, L0_tok_b, L0_tok_class_token, L0_tok_pos_emb)
    h = jnp.concatenate([h, txt], axis=1)
    h = h + _L0_attn_ref(_layernorm(h, axis=-1), L0_attn_f_in, L0_attn_f_cw, L0_attn_f_cb, L0_attn_f_xp, L0_attn_f_dtw, L0_attn_f_dtb, L0_attn_f_Alog, L0_attn_f_D, L0_attn_f_out, L0_attn_b_in, L0_attn_b_cw, L0_attn_b_cb, L0_attn_b_xp, L0_attn_b_dtw, L0_attn_b_dtb, L0_attn_b_Alog, L0_attn_b_D, L0_attn_b_out, L0_attn_ln_g, L0_attn_ln_b)
    h = h + _L0_ffn_ref(_layernorm(h, axis=-1), L0_ffn_gumbel_weights, L0_ffn_n1l_g, L0_ffn_n1l_b, L0_ffn_n1s_g, L0_ffn_n1s_b, L0_ffn_w_qkv, L0_ffn_w_proj, L0_ffn_b_proj, L0_ffn_n2l_g, L0_ffn_n2l_b, L0_ffn_n2s_g, L0_ffn_n2s_b, L0_ffn_w_fc1, L0_ffn_b_fc1, L0_ffn_w_fc2, L0_ffn_b_fc2)
    return h

_drawn_inputs = setup_inputs


def setup_inputs(seed=0):
    import zlib

    import numpy as np

    out = dict(_drawn_inputs(seed))
    spreads = {'L0_tok_b': (0.0, 0.1),
     'L0_attn_f_D': (1.0, 0.2),
     'L0_attn_b_D': (1.0, 0.2),
     'L0_attn_ln_g': (1.0, 0.2),
     'L0_attn_ln_b': (0.0, 0.1),
     'L0_ffn_n1l_g': (1.0, 0.6),
     'L0_ffn_n1l_b': (0.0, 0.8),
     'L0_ffn_n1s_g': (1.0, 0.6),
     'L0_ffn_n1s_b': (0.0, 0.8),
     'L0_ffn_b_proj': (0.0, 0.1),
     'L0_ffn_n2l_g': (1.0, 0.6),
     'L0_ffn_n2l_b': (0.0, 2.0),
     'L0_ffn_n2s_g': (1.0, 0.6),
     'L0_ffn_n2s_b': (0.0, 2.0),
     'L0_ffn_b_fc1': (0.0, 0.8),
     'L0_ffn_b_fc2': (0.0, 0.1)}
    factors = {'L0_attn_f_cb': 6.508,
     'L0_attn_f_dtb': 5.329,
     'L0_attn_f_Alog': 2.675,
     'L0_attn_b_cb': 6.387,
     'L0_attn_b_dtb': 4.997,
     'L0_attn_b_Alog': 2.874,
     'L0_ffn_gumbel_weights': 6.998,
     'L0_ffn_w_qkv': 3.536,
     'L0_ffn_w_proj': 3.441}
    for name, (base, spread) in spreads.items():
        noise = np.random.default_rng([zlib.crc32(name.encode()), seed]).standard_normal(out[name].shape)
        drawn = base * np.exp(spread * noise) if base else spread * noise
        out[name] = jnp.asarray(drawn.astype(out[name].dtype))
    for name, factor in factors.items():
        out[name] = (out[name] * factor).astype(out[name].dtype)
    return out
```

```python
from contextlib import ExitStack

import concourse.bass as bass
from concourse import mybir

F32 = mybir.dt.float32
BF16 = mybir.dt.bfloat16
ALU = mybir.AluOpType
ACT = mybir.ActivationFunctionType
AX_X = mybir.AxisListType.X

BATCH = 32
LARGE = BATCH // 2
PATCHES = 196
PD = 768
KP = PD // 128
TXT = 77
T = 1 + PATCHES + TXT
C = 192
CH = C // 2
INNER = 384
IC = INNER // 128
N = 16
NH = N // 2
RANK = 12
TAPS = 4
PAD = TAPS - 1
XI_W = T + 2 * PAD
UNITS = 2 * IC
SCANS = 2 * UNITS
HEADS = 12
HD = C // HEADS
GROUPS = HEADS // 4
QS = (0, 91, 182)
QT = 92
HID = 4 * C
HC = HID // 128
EPS = 1e-5
GAPS = 18

(P_TOKB, P_CLS, P_LNG, P_LNB, P_N1LG, P_N1LB, P_N1SG, P_N1SB, P_N2LG, P_N2LB, P_N2SG, P_N2SB,
 P_BPROJ, P_BFC2) = range(14)
P_POS = 14
FEAT_W = P_POS + 1 + PATCHES
I_CB, I_D, I_A = TAPS, TAPS + 1, TAPS + 2
INNER_W = I_A + N


def ago(b, m):
    return (b[0], b[1] - m)


def parity(b):
    return b[1] % 2


def first(b):
    return isinstance(b[0], int) and b[1] == 0


def last(b):
    return isinstance(b[0], int) and b[1] == BATCH - 1


def number(b):
    return b[0] * 2 + b[1]


def at(b, per_batch, n):
    return b[0] * (2 * per_batch) + (b[1] * per_batch + n)


def uneven(b, small, per_large, per_small, n):
    if not small:
        return at(b, per_large, n)
    return at(b, per_small, n - LARGE * (per_small - per_large))


def mlp_at(b, small, n):
    return uneven(b, small, HC, 3 * HC, n)


def every_other(b, n):
    return b[0] * n + (b[1] // 2 + 1) * n


def wait(eng, sem, value):
    if isinstance(value, int) and value <= 0:
        return
    eng.wait_ge(sem, value)


def build(nc, patches, txt, tok_w, feat, w_in, inner, x_proj, dt_w, w_out, w_qk, w_v, w_proj,
          fc1, fc1_b, fc2, gumbel, out):
    with ExitStack() as ctx:
        def sb(name, shape, dt=F32):
            return ctx.enter_context(nc.sbuf_tensor(name, shape, dt))

        def sem(name):
            return ctx.enter_context(nc.semaphore(name))

        tok_w_s = sb("tok_w_s", [128, KP, C])
        feat_s = sb("feat_s", [CH, 2, FEAT_W])
        w_in_s = sb("w_in_s", [CH, 2, 2, 2 * INNER])
        inner_s = sb("inner_s", [128, 2, IC, INNER_W])
        x_proj_s = sb("x_proj_s", [128, 2, IC, 128])
        dt_w_s = sb("dt_w_s", [RANK + 1, 2, INNER])
        w_out_s = sb("w_out_s", [128, 2, IC, C])
        w_qk_s = sb("w_qk_s", [CH, 2, 2, GROUPS * 128])
        w_v_s = sb("w_v_s", [CH, 2, C + HD])
        w_proj_s = sb("w_proj_s", [128, GROUPS, C])
        fc1_s = sb("fc1_s", [CH, 2, HID])
        fc1_b_s = sb("fc1_b_s", [128, HC])
        fc2_s = sb("fc2_s", [128, HC, C])
        gate = sb("gate", [CH, 3])
        bias_sum = sb("bias_sum", [CH, 2, 2])
        gate_sum = sb("gate_sum", [CH, 2])
        ident = sb("ident", [128, 128])
        mean_w = sb("mean_w", [CH, CH])
        pick = sb("pick", [128, 32], BF16)
        v_mask = sb("v_mask", [QT, 3])
        eps_c = sb("eps_c", [128, 1])
        one_c = sb("one_c", [128, 1])

        xp = sb("xp", [128, KP, PATCHES])
        h = [sb(f"h{i}", [CH, 2, T]) for i in range(2)]
        xn = [sb(f"xn{i}", [CH, 2, T]) for i in range(2)]
        h2 = sb("h2", [CH, 2, T])
        res = sb("res", [CH, 2, T])
        cen = sb("cen", [CH, 2, T])
        rstd_a = sb("rstd_a", [CH, T])
        rstd_f = sb("rstd_f", [CH, T])
        xi = sb("xi", [128, IC, XI_W])
        zs = [sb(f"zs{d}", [128, IC, T]) for d in range(2)]
        xc = [sb(f"xc{d}", [128, IC, T]) for d in range(2)]
        dt = [sb(f"dt{d}", [128, IC, T]) for d in range(2)]
        dtu = [sb(f"dtu{d}", [128, IC, T]) for d in range(2)]
        parts = sb("parts", [128, T], BF16)
        dt_lo = sb("dt_lo", [RANK + 1, T])
        states = [sb(f"b_rows{i}", [128, NH, T]) for i in range(2)]
        reads = [sb(f"c_rows{i}", [128, NH, T]) for i in range(2)]
        decay = [sb(f"decay{i}", [128, NH, T]) for i in range(2)]
        hs = [sb(f"hs{i}", [128, NH, T]) for i in range(2)]
        yg = sb("yg", [128, UNITS, T])
        qk = sb("qk", [128, 2, T])
        v_s = sb("v_s", [QT, 3, C + HD])
        prob = [sb(f"prob{i}", [QT, 3, T]) for i in range(2)]
        prob_t = sb("prob_t", [QT, 4, 3, T])
        neg_max = sb("neg_max", [QT, 2, 3])
        row_max = sb("row_max", [QT, 2, 3])
        row_sum = sb("row_sum", [QT, 2, 3])
        row_inv = sb("row_inv", [QT, 2, 3])
        o_s = sb("o_s", [128, GROUPS, T])
        hid = sb("hid", [128, 2, T])
        sq_a = xp[0:CH, 0:3, :].rearrange("p a t -> p (a t)")[:, 0:2 * T].rearrange("p (a t) -> p a t", a=2)
        sq_f = hid[0:CH, :, :]

        y_ps = ctx.enter_context(nc.psum_tensor("y_ps", [128, 512], F32))
        a_ps = ctx.enter_context(nc.psum_tensor("a_ps", [128, 2, 512], F32))
        f_ps = ctx.enter_context(nc.psum_tensor("f_ps", [128, 5, 512], F32))

        s_w = sem("weights_loaded")
        s_c = sem("constants_made")
        s_cp = sem("constants_pool")
        s_ca = sem("constants_act")
        s_x = sem("patches_loaded")
        s_txt = [sem(f"txt_loaded{i}") for i in range(2)]
        tok_mm = sem("tok_mm")
        h_ready = sem("h_ready")
        a_mean = sem("a_mean")
        a_cen = sem("a_cen")
        a_sq = sem("a_sq")
        a_var = sem("a_var")
        a_ln = sem("a_ln")
        a_rstd = sem("a_rstd")
        xn_ready = sem("xn_ready")
        xz_mm = sem("xz_mm")
        xz_copied = sem("xz_copied")
        conv_tap = sem("conv_tap")
        silu_done = sem("silu_done")
        xp_mm = sem("xproj_mm")
        xp_hi = sem("xproj_hi")
        dtlo_ready = sem("dtlo_ready")
        split = sem("split")
        dtv_mm = sem("dtv_mm")
        dtv_abs = sem("dtv_abs")
        dtv_max = sem("dtv_max")
        sp_exp = sem("softplus_exp")
        sp_ln = sem("softplus_ln")
        dt_ready = sem("dt_ready")
        dtu_ready = sem("dtu_ready")
        bc_mm = sem("bc_mm")
        bc_copied = sem("bc_copied")
        a_neg = sem("a_negated")
        edge = sem("edge_zeroed")
        exp_done = sem("exp_done")
        dbu_done = sem("dbu_done")
        scan_done = sem("scan_done")
        hc_done = sem("hc_done")
        ysum = sem("ysum")
        gate_tmp = sem("gate_tmp")
        gated = sem("gated")
        out_mm = sem("out_mm")
        r_ready = sem("r_ready")
        f_mean = sem("f_mean")
        f_cen = sem("f_cen")
        f_sq = sem("f_sq")
        f_var = sem("f_var")
        f_ln = sem("f_ln")
        f_rstd = sem("f_rstd")
        f_y = sem("f_y")
        f_aff = sem("f_affine")
        h2_tmp = sem("h2_tmp")
        h2_ready = sem("h2_ready")
        qk_mm = sem("qk_mm")
        qk_copied = sem("qk_copied")
        v_mm = sem("v_mm")
        v_copied = sem("v_copied")
        sc_mm = sem("scores_mm")
        mx_done = sem("mx_done")
        nmx_done = sem("nmx_done")
        pexp = sem("prob_exp")
        inv_done = sem("inv_done")
        p_norm = sem("prob_normed")
        pt_mm = sem("prob_t_mm")
        pt_copied = sem("prob_t_copied")
        av_mm = sem("av_mm")
        av_copied = sem("av_copied")
        pr_mm = sem("proj_mm")
        x3_step = sem("x3_step")
        fc1_mm = sem("fc1_mm")
        gelu_done = sem("gelu_done")
        fc2_mm = sem("fc2_mm")
        fin_step = sem("fin_step")
        out_ready = sem("out_ready")
        out_stored = sem("out_stored")

        LOADS = [(tok_w_s, tok_w), (feat_s, feat), (w_in_s, w_in), (inner_s, inner), (x_proj_s, x_proj),
                 (dt_w_s, dt_w), (w_out_s, w_out), (w_qk_s, w_qk), (w_v_s, w_v), (w_proj_s, w_proj),
                 (fc1_s, fc1), (fc1_b_s, fc1_b), (fc2_s, fc2), (gate, gumbel)]
        CONSTS = 18
        BC_GAPS = (13, 15, 16, 17)

        block = ctx.enter_context(nc.Block())

        def program(step, gaps_loop, front, finish):
            front()
            step((0, 0), None, (0, 1), False)
            step((0, 1), (0, 0), (0, 2), False)
            step((0, 2), (0, 1), (0, 3), False)
            with gaps_loop(1, LARGE // 2) as r:
                for off in (1, 2):
                    step((r, off), (r, off - 1), (r, off + 1), False)
            with gaps_loop(LARGE // 2, BATCH // 2 - 1) as r:
                for off in (1, 2):
                    step((r, off), (r, off - 1), (r, off + 1), True)
            step((0, BATCH - 1), (0, BATCH - 2), None, True)
            finish((0, BATCH - 1))

        @block.sync
        def _(sp):
            def load_patches(b):
                wait(sp, a_var, at(b, 1, 0))
                wait(sp, tok_mm, at(b, 1, 0))
                sp.dma_start(xp[:, :, :], patches[number(b)]).then_inc(s_x, 16)

            def load_txt(b):
                wait(sp, h2_ready, at(ago(b, 1), 1, 0))
                sp.dma_start(h[parity(b)][:, :, 1 + PATCHES:T], txt[number(b)]).then_inc(s_txt[parity(b)], 16)

            def store(b):
                sp.wait_ge(out_ready, at(b, 1, 1))
                sp.dma_start(out[number(b)], h2[:, :, :]).then_inc(out_stored, 16)

            def front():
                load_patches((0, 0))
                load_txt((0, 0))
                for dst, src in LOADS:
                    sp.dma_start(dst[tuple(slice(None) for _ in dst.shape)], src).then_inc(s_w, 16)

            def step(b, f, a, small):
                if a is not None:
                    load_patches(a)
                    load_txt(a)
                if f is not None:
                    store(f)

            def finish(f):
                store(f)
                sp.wait_ge(out_stored, at(f, 16, 16))

            program(step, sp.Fori, front, finish)

        @block.gpsimd
        def _(pool):
            pool.memset(ident[:, :], 0.0).then_inc(s_cp, 1)
            pool.memset(pick[:, :], 0.0).then_inc(s_cp, 1)
            pool.memset(v_mask[:, :], 1.0).then_inc(s_cp, 1)
            pool.wait_ge(s_cp, 3)
            pool.affine_select(out=ident[:, :], in_=ident[:, :], compare_op=ALU.not_equal, fill=1.0, base=0,
                               pattern=[[-1, 128]], channel_multiplier=1).then_inc(s_cp, 1)
            for q in (1, 2, 3):
                pool.affine_select(out=pick[:, :], in_=pick[:, :], compare_op=ALU.not_equal, fill=1.0,
                                   base=-32 * q, pattern=[[-1, 32]], channel_multiplier=1).then_inc(s_cp, 1)
                pool.wait_ge(s_cp, 4 + q)
            pool.memset(v_mask[0:1, 1:3], 0.0).then_inc(s_cp, 1)

        @block.tensor
        def _(pe):
            def mean_mm(bank, x, done):
                for i in range(2):
                    mm = pe.matmul(bank[0:CH, 0:T], mean_w[:, :], x[:, i, :], start=(i == 0), stop=(i == 1))
                mm.then_inc(done, 1)

            def ysum_part(b, q, lo, hi, between=None):
                if lo == 0:
                    wait(pe, hc_done, at(b, SCANS, q + 1))
                    if q % 2 == 0:
                        wait(pe, gate_tmp, at(b, UNITS, q // 2))
                for n in range(lo, hi):
                    mm = pe.matmul(y_ps[:, 0:T], ident[:, :], hs[q % 2][:, n, :],
                                   start=(q % 2 == 0 and n == 0), stop=(q % 2 == 1 and n == NH - 1))
                    if n == NH - 1:
                        mm.then_inc(ysum, 1)
                    if between:
                        between()

            def tok(b):
                pe.wait_ge(s_x, at(b, 16, 16))
                wait(pe, dtv_abs, at(b, 6, 0))
                wait(pe, dtv_max, at(b, 6, 0))
                for i in range(2):
                    for k in range(KP):
                        mm = pe.matmul(a_ps[0:CH, 0, i * PATCHES:(i + 1) * PATCHES],
                                       tok_w_s[:, k, i * CH:(i + 1) * CH], xp[:, k, :],
                                       start=(k == 0), stop=(k == KP - 1))
                mm.then_inc(tok_mm, 1)

            def a_mean_mm(b):
                pe.wait_ge(h_ready, at(b, 1, 1))
                pe.wait_ge(s_txt[parity(b)], every_other(b, 16))
                mean_mm(a_ps[:, 1, :], h[parity(b)], a_mean)

            def a_var_mm(b):
                pe.wait_ge(a_sq, at(b, 1, 1))
                mean_mm(a_ps[:, 1, :], sq_a, a_var)

            def in_proj(b, d, lo, hi):
                if lo == 0:
                    pe.wait_ge(xn_ready, at(b, 1, 1))
                    wait(pe, bc_copied, at(b, 64, 32 * d))
                for j in range(lo, hi):
                    if j >= 2:
                        pe.wait_ge(xz_copied, at(b, 12, 6 * d + j - 1))
                    for i in range(2):
                        mm = pe.matmul(a_ps[:, j % 2, 0:T], w_in_s[:, i, d, j * 128:(j + 1) * 128],
                                       xn[parity(b)][:, i, :], start=(i == 0), stop=(i == 1))
                    mm.then_inc(xz_mm, 1)

            def x_proj_mm(b, d):
                pe.wait_ge(xz_copied, at(b, 12, 6 * d + 6))
                pe.wait_ge(silu_done, at(b, 4, 2 * d + 1))
                for k in range(IC):
                    mm = pe.matmul(a_ps[:, 0, 0:T], x_proj_s[:, d, k, :], xc[d][:, k, :],
                                   start=(k == 0), stop=(k == IC - 1))
                mm.then_inc(xp_mm, 1)

            def dt_mm(b, d):
                pe.wait_ge(dtlo_ready, at(b, 2, d + 1))
                for j in range(IC):
                    bank = (j + 1) % 2
                    if j == 1:
                        pe.wait_ge(split, at(b, 6, 3 * d + 3))
                    if j == 2:
                        pe.wait_ge(dtv_abs, at(b, 6, 3 * d + 1))
                        pe.wait_ge(dtv_max, at(b, 6, 3 * d + 1))
                    pe.matmul(a_ps[:, bank, 0:T], dt_w_s[:, d, j * 128:(j + 1) * 128], dt_lo[:, :],
                              start=True, stop=True).then_inc(dtv_mm, 1)

            def bc_row(b, d, i):
                if i == 0:
                    pe.wait_ge(dtv_abs, at(b, 6, 3 * d + 3))
                    pe.wait_ge(dtv_max, at(b, 6, 3 * d + 3))
                    if d == 1 and not last(b):
                        pe.wait_ge(h_ready, at(b, 1, 2))
                if i == 1 and d == 1 and not last(b):
                    pe.wait_ge(a_ln, at(b, 1, 2))
                if i >= 2:
                    pe.wait_ge(bc_copied, at(b, 64, 32 * d + i - 1))
                kind, half, n = (i // 8) % 2, i // 16, i % 8
                row = N * kind + NH * half + n
                pe.matmul(a_ps[:, i % 2, 0:T], pick[:, row:row + 1].broadcast_to([128, 128]), parts[:, :],
                          start=True, stop=True).then_inc(bc_mm, 1)

            def out_proj(f):
                pe.wait_ge(gated, at(f, UNITS, UNITS))
                wait(pe, out_ready, at(f, 1, 0))
                for i in range(2):
                    for u in range(UNITS):
                        mm = pe.matmul(f_ps[0:CH, i, 0:T], w_out_s[:, u // IC, u % IC, i * CH:(i + 1) * CH],
                                       yg[:, u, :], start=(u == 0), stop=(u == UNITS - 1))
                mm.then_inc(out_mm, 1)

            def f_mean_mm(f, j, x, ready, value):
                pe.wait_ge(ready, value)
                mean_mm(f_ps[:, 2, :], x, f_mean)

            def f_var_mm(f, j):
                pe.wait_ge(f_sq, at(f, 4, j + 1))
                mean_mm(f_ps[:, 3, :], sq_f, f_var)

            def qk_mms(f, g):
                if g == 0:
                    pe.wait_ge(f_aff, at(f, 2, 1))
                else:
                    pe.wait_ge(pexp, at(f, HEADS, 4 * g))
                for s in range(2):
                    for i in range(2):
                        mm = pe.matmul(f_ps[:, s, 0:T], w_qk_s[:, i, s, g * 128:(g + 1) * 128], cen[:, i, :],
                                       start=(i == 0), stop=(i == 1))
                    mm.then_inc(qk_mm, 1)

            def v_mms(f):
                for t in range(3):
                    for i in range(2):
                        mm = pe.matmul(f_ps[0:QT, 2 + t, 0:C + HD], cen[:, i, QS[t]:QS[t] + QT], w_v_s[:, i, :],
                                       start=(i == 0), stop=(i == 1))
                    mm.then_inc(v_mm, 1)

            def scores(f, hd):
                g, r = hd // 4, 32 * (hd % 4)
                pe.wait_ge(qk_copied, at(f, 2 * GROUPS, 2 * g + 2))
                if hd == 0:
                    pe.wait_ge(v_copied, at(f, 3, 3))
                else:
                    pe.wait_ge(pexp, at(f, HEADS, hd))
                for t in range(3):
                    mm = pe.matmul(f_ps[0:QT, t, 0:T], qk[r:r + HD, 0, QS[t]:QS[t] + QT], qk[r:r + HD, 1, :],
                                   start=True, stop=True)
                mm.then_inc(sc_mm, 1)

            def turn(f, hd):
                pe.wait_ge(p_norm, at(f, HEADS, hd + 1))
                for t in range(3):
                    n = 3 * hd + t
                    if n >= 2:
                        pe.wait_ge(pt_copied, at(f, 3 * HEADS, n - 1))
                    if n in (12, 24):
                        pe.wait_ge(av_copied, at(f, GROUPS, n // 12))
                    for k in range(3):
                        mm = pe.transpose(f_ps[0:QT, 3 + n % 2, k * QT:(k + 1) * QT],
                                          prob[hd % 2][:, t, QS[k]:QS[k] + QT], ident[0:QT, 0:QT])
                    mm.then_inc(pt_mm, 1)

            def av(f, g):
                pe.wait_ge(pt_copied, at(f, 3 * HEADS, 12 * g + 12))
                for k in range(3):
                    for r in range(4):
                        hd = 4 * g + r
                        mm = pe.matmul(f_ps[32 * r:32 * r + 32, 3, 0:T], v_s[:, k, hd * HD:hd * HD + 2 * HD],
                                       prob_t[:, r, k, :], start=(k == 0), stop=(k == 2),
                                       skip_group_check=True)
                mm.then_inc(av_mm, 1)

            def proj(f, small):
                pe.wait_ge(av_copied, at(f, GROUPS, GROUPS))
                for i in range(2):
                    for g in range(GROUPS):
                        mm = pe.matmul(f_ps[0:CH, i, 0:T], w_proj_s[:, g, i * CH:(i + 1) * CH], o_s[:, g, :],
                                       start=(g == 0), stop=(g == GROUPS - 1))
                if small:
                    pe.matmul(f_ps[0:CH, 2, 0:T], w_proj_s[:, 0, 0:CH], o_s[:, 0, :], start=True, stop=False)
                    pe.matmul(f_ps[0:CH, 2, 0:T], w_proj_s[0:64, 1, 0:CH], o_s[0:64, 1, :],
                              start=False, stop=True)
                    mm = pe.matmul(f_ps[0:CH, 3, 0:T], w_proj_s[:, 0, 0:CH], o_s[:, 0, :], start=True, stop=True)
                mm.then_inc(pr_mm, 1)

            def mlp(f, small, lo, hi):
                chunks = 3 * HC if small else HC
                for q in range(lo, hi):
                    if q < chunks:
                        v, ch = q // HC, q % HC
                        if q == 0:
                            pe.wait_ge(f_aff, at(f, 2, 2))
                        if q >= 2:
                            pe.wait_ge(gelu_done, mlp_at(f, small, q - 1))
                        keep = [(CH, 2), (CH, 1), (C // 3, 1)][v]
                        for i in range(keep[1]):
                            mm = pe.matmul(f_ps[:, q % 2, 0:T], fc1_s[0:keep[0], i, ch * 128:(ch + 1) * 128],
                                           cen[0:keep[0], i, :], start=(i == 0), stop=(i == keep[1] - 1))
                        mm.then_inc(fc1_mm, 1)
                    if q >= 1:
                        p = q - 1
                        v, ch = p // HC, p % HC
                        pe.wait_ge(gelu_done, mlp_at(f, small, p + 1))
                        if p == 2 * HC:
                            pe.wait_ge(fin_step, uneven(f, True, 2, 6, 1))
                        for i, bank in [[(0, 3), (1, 4)], [(0, 2)], [(0, 3)]][v]:
                            mm = pe.matmul(f_ps[0:CH, bank, 0:T], fc2_s[:, ch, i * CH:(i + 1) * CH],
                                           hid[:, p % 2, :], start=(ch == 0), stop=(ch == HC - 1))
                        mm.then_inc(fc2_mm, 1)

            def fine(f, gap, small):
                if gap == 4:
                    out_proj(f)
                if gap == 6:
                    f_mean_mm(f, 0, res, r_ready, at(f, 1, 1))
                if gap in (7, 9, 11, 30):
                    f_var_mm(f, (7, 9, 11, 30).index(gap))
                if gap == 8:
                    f_mean_mm(f, 1, h2, h2_ready, at(f, 1, 1))
                if gap == 10:
                    f_mean_mm(f, 2, res, f_y, at(f, 4, 2))
                if gap == 12:
                    qk_mms(f, 0)
                    v_mms(f)
                if 14 <= gap < 14 + HEADS:
                    if gap in (18, 22):
                        qk_mms(f, (gap - 14) // 4)
                    scores(f, gap - 14)
                if 16 <= gap < 16 + HEADS:
                    turn(f, gap - 16)
                    if gap in (19, 23, 27):
                        av(f, (gap - 19) // 4)
                if gap == 28:
                    proj(f, small)
                if gap == 29:
                    f_mean_mm(f, 3, res, x3_step, uneven(f, small, 2, 6, 6 if small else 2))
                if gap >= 31:
                    per, end = (4, 3 * HC + 1) if small else (2, HC + 1)
                    mlp(f, small, min(per * (gap - 31), end), min(per * (gap - 30), end))

            def fronts(b, d, a, gap):
                x, xd = (b, 1) if d == 0 else (a, 0)
                if x is not None:
                    if gap == 1:
                        in_proj(x, xd, 0, IC)
                    if gap == 4:
                        in_proj(x, xd, IC, 2 * IC)
                    if gap == 7:
                        x_proj_mm(x, xd)
                    if gap == 9:
                        dt_mm(x, xd)
                if d == 0 and a is not None:
                    if gap == 9:
                        tok(a)
                    if gap == 10:
                        a_mean_mm(a)
                    if gap == 12:
                        a_var_mm(a)

            def step(b, f, a, small):
                for d in range(2):
                    x, xd = (b, 1) if d == 0 else (a, 0)
                    for gap in range(GAPS):
                        q = d * 6 + gap // 3 - 1
                        rows = None
                        if gap in BC_GAPS and x is not None:
                            rows = iter(range(8 * BC_GAPS.index(gap), 8 * BC_GAPS.index(gap) + 8))

                        def between():
                            for _ in range(3):
                                i = next(rows, None)
                                if i is not None:
                                    bc_row(x, xd, i)

                        lo, hi = [(0, 3), (3, 6), (6, 8)][gap % 3]
                        if q >= 0:
                            ysum_part(b, q, lo, hi, between if rows is not None else None)
                        elif not first(b):
                            ysum_part(ago(b, 1), SCANS - 1, lo, hi)
                        if rows is not None:
                            for i in rows:
                                bc_row(x, xd, i)
                        if f is not None:
                            fine(f, d * GAPS + gap, small)
                        fronts(b, d, a, gap)

            def front():
                pe.wait_ge(s_w, 16 * len(LOADS))
                pe.wait_ge(s_cp, 8)
                pe.wait_ge(s_c, CONSTS)
                b = (0, 0)
                tok(b)
                a_mean_mm(b)
                a_var_mm(b)
                in_proj(b, 0, 0, 6)
                x_proj_mm(b, 0)
                dt_mm(b, 0)
                for i in range(32):
                    bc_row(b, 0, i)

            def finish(f):
                ysum_part(f, SCANS - 1, 0, NH)
                for gap in range(2 * GAPS):
                    fine(f, gap, True)

            program(step, pe.Fori, front, finish)

        @block.scalar
        def _(act):
            def exps(b, q, lo, hi):
                d, u, half = q // 6, (q // 2) % IC, q % 2
                if lo == 0:
                    act.wait_ge(dt_ready, at(b, 4, 2 * d + 2))
                    wait(act, scan_done, at(b, SCANS, q - 1))
                for n in range(lo, hi):
                    s = I_A + NH * half + n
                    t = slice(1, T) if d == 0 else slice(0, T - 1)
                    e = act.activation(decay[half][:, n, t], dt[d][:, u, t], ACT.Exp,
                                       scale=inner_s[:, d, u, s:s + 1])
                if hi == NH:
                    e.then_inc(exp_done, 1)

            def squares(x, out, ready, value, done):
                act.wait_ge(ready, value)
                act.activation(out, x, ACT.Square).then_inc(done, 1)

            def rstd(bank, out, ready, value, ln_sem, ln_value, done):
                act.wait_ge(ready, value)
                act.activation(out[:, :], bank, ACT.Ln, bias=eps_c[0:CH, 0:1]).then_inc(ln_sem, 1)
                act.wait_ge(ln_sem, ln_value)
                act.activation(out[:, :], out[:, :], ACT.Exp, scale=-0.5).then_inc(done, 1)

            def xz_copy(b, d, lo, hi):
                for j in range(lo, hi):
                    act.wait_ge(xz_mm, at(b, 12, 6 * d + j + 1))
                    if j == 0:
                        wait(act, conv_tap, at(b, 24, 12 * d))
                    if j == IC:
                        wait(act, gated, at(ago(b, 1), UNITS, IC * (d + 1)))
                    dst = xi[:, j, PAD:PAD + T] if j < IC else zs[d][:, j - IC, :]
                    act.activation(dst, a_ps[:, j % 2, 0:T], ACT.Copy).then_inc(xz_copied, 1)

            def silu(b, d):
                act.wait_ge(conv_tap, at(b, 24, 12 * d + 12))
                act.wait_ge(xz_copied, at(b, 12, 6 * d + 6))
                act.activation(xc[d][:, :, :], xc[d][:, :, :], ACT.Silu).then_inc(silu_done, 1)
                act.activation(zs[d][:, :, :], zs[d][:, :, :], ACT.Silu).then_inc(silu_done, 1)
                act.preload_act_table_set("natural_log_exp_and_others")

            def xproj_copy(b, d):
                act.wait_ge(xp_mm, at(b, 2, d + 1))
                wait(act, dtv_mm, at(b, 6, 3 * d))
                act.activation(dt_lo[0:RANK, :], a_ps[0:RANK, 0, 0:T], ACT.Copy).then_inc(dtlo_ready, 1)
                wait(act, bc_mm, at(b, 64, 32 * d))
                act.activation(parts[:, :], a_ps[:, 0, 0:T], ACT.Copy).then_inc(xp_hi, 1)

            def softplus(b, d):
                for j in range(IC):
                    act.wait_ge(dtv_mm, at(b, 6, 3 * d + j + 1))
                    act.activation(dtu[d][:, j, :], a_ps[:, (j + 1) % 2, 0:T], ACT.Abs).then_inc(dtv_abs, 1)
                act.wait_ge(dtv_abs, at(b, 6, 3 * d + 3))
                act.activation(dtu[d][:, :, :], dtu[d][:, :, :], ACT.Exp, scale=-1.0).then_inc(sp_exp, 1)
                act.wait_ge(sp_exp, at(b, 2, d + 1))
                act.activation(dtu[d][:, :, :], dtu[d][:, :, :], ACT.Ln, bias=one_c[:, 0:1]).then_inc(sp_ln, 1)

            def bc_copy(b, d, blk):
                last = SCANS - 2 if d == 0 else SCANS // 2 - 2
                used = (dbu_done, hc_done, dbu_done, hc_done)[blk]
                prev = ago(b, 1) if d == 0 else b
                wait(act, used, at(prev, SCANS, last + 1 + blk // 2))
                dst = (states[0], reads[0], states[1], reads[1])[blk]
                for i in range(8):
                    act.wait_ge(bc_mm, at(b, 64, 32 * d + 8 * blk + i + 1))
                    act.activation(dst[:, i, :], a_ps[:, i % 2, 0:T], ACT.Copy).then_inc(bc_copied, 1)

            def qk_copy(f, g):
                for s in range(2):
                    act.wait_ge(qk_mm, at(f, 2 * GROUPS, 2 * g + s + 1))
                    if s == 0:
                        wait(act, sc_mm, at(f, HEADS, 4 * g))
                    act.activation(qk[:, s, :], f_ps[:, s, 0:T], ACT.Copy).then_inc(qk_copied, 1)

            def v_copy(f):
                for t in range(3):
                    act.wait_ge(v_mm, at(f, 3, t + 1))
                    if t == 0:
                        wait(act, av_mm, at(f, GROUPS, 0))
                    act.activation(v_s[:, t, :], f_ps[0:QT, 2 + t, 0:C + HD], ACT.Copy,
                                   scale=v_mask[:, t:t + 1]).then_inc(v_copied, 1)

            def softmax_exp(f, hd):
                act.wait_ge(nmx_done, at(f, HEADS, hd + 1))
                wait(act, pt_mm, at(f, 3 * HEADS, 3 * hd - 3))
                for t in range(3):
                    e = act.activation(prob[hd % 2][:, t, :], f_ps[0:QT, t, 0:T], ACT.Exp, scale=HD ** -0.5,
                                       bias=neg_max[:, hd % 2, t:t + 1], accum_out=row_sum[:, hd % 2, t:t + 1])
                e.then_inc(pexp, 1)

            def turn_copy(f, hd):
                if hd % 4 == 0:
                    wait(act, av_mm, at(f, GROUPS, hd // 4))
                for t in range(3):
                    n = 3 * hd + t
                    act.wait_ge(pt_mm, at(f, 3 * HEADS, n + 1))
                    new = min(t, 1)
                    act.activation(prob_t[:, hd % 4, :, QS[t] + new:QS[t] + QT],
                                   f_ps[0:QT, 3 + n % 2, 0:3 * QT].rearrange("p (k t) -> p k t", k=3)[:, :, new:],
                                   ACT.Copy).then_inc(pt_copied, 1)

            def av_copy(f, g):
                act.wait_ge(av_mm, at(f, GROUPS, g + 1))
                if g == 0:
                    wait(act, pr_mm, at(f, 1, 0))
                act.activation(o_s[:, g, :], f_ps[:, 3, 0:T], ACT.Copy).then_inc(av_copied, 1)

            def gelus(f, small, lo, hi):
                for q in range(lo, hi):
                    act.wait_ge(fc1_mm, mlp_at(f, small, q + 1))
                    if q >= 2:
                        act.wait_ge(fc2_mm, mlp_at(f, small, q - 1))
                    act.activation(hid[:, q % 2, :], f_ps[:, q % 2, 0:T], ACT.Gelu,
                                   bias=fc1_b_s[:, q % HC:q % HC + 1]).then_inc(gelu_done, 1)

            def fine(f, gap, small):
                if gap in (7, 9, 11, 30):
                    j = (7, 9, 11, 30).index(gap)
                    squares(cen[:, :, :] if j != 1 else res[:, :, :], sq_f, f_cen, at(f, 4, j + 1), f_sq)
                    rstd(f_ps[0:CH, 3, 0:T], rstd_f, f_var, at(f, 4, j + 1), f_ln, at(f, 4, j + 1), f_rstd)
                if gap == 12:
                    qk_copy(f, 0)
                    v_copy(f)
                if 15 <= gap < 15 + HEADS:
                    softmax_exp(f, gap - 15)
                if gap in (18, 22):
                    qk_copy(f, (gap - 14) // 4)
                if 16 <= gap < 16 + HEADS:
                    turn_copy(f, gap - 16)
                    if gap in (19, 23, 27):
                        av_copy(f, (gap - 19) // 4)
                if gap >= 31:
                    chunks = 3 * HC if small else HC
                    per = 4 if small else 2
                    gelus(f, small, min(per * (gap - 31), chunks), min(per * (gap - 30), chunks))
                    if gap == 35:
                        act.preload_act_table_set("natural_log_exp_and_others")

            def fronts(b, d, a, gap):
                x, xd = (b, 1) if d == 0 else (a, 0)
                if x is not None:
                    if gap == 1:
                        xz_copy(x, xd, 0, IC)
                    if gap == 4:
                        xz_copy(x, xd, IC, 2 * IC)
                    if gap == 6:
                        silu(x, xd)
                    if gap == 7:
                        xproj_copy(x, xd)
                    if gap == 9:
                        softplus(x, xd)
                if d == 0 and a is not None:
                    if gap == 11:
                        squares(xn[parity(a)][:, :, :], sq_a, a_cen, at(a, 1, 1), a_sq)
                    if gap == 12:
                        rstd(a_ps[0:CH, 1, 0:T], rstd_a, a_var, at(a, 1, 1), a_ln, at(a, 1, 1), a_rstd)

            def step(b, f, a, small):
                for d in range(2):
                    x, xd = (b, 1) if d == 0 else (a, 0)
                    for gap in range(GAPS):
                        if gap in BC_GAPS and x is not None:
                            bc_copy(x, xd, BC_GAPS.index(gap))
                        q = d * 6 + gap // 3 + 1
                        lo, hi = [(0, 3), (3, 6), (6, 8)][gap % 3]
                        if q < SCANS:
                            exps(b, q, lo, hi)
                        elif a is not None:
                            exps(a, 0, lo, hi)
                        if f is not None:
                            fine(f, d * GAPS + gap, small)
                        fronts(b, d, a, gap)

            def front():
                act.wait_ge(s_w, 16 * len(LOADS))
                act.wait_ge(s_cp, 8)
                act.wait_ge(s_c, CONSTS)
                act.preload_act_table_set("natural_log_exp_and_others")
                act.activation(inner_s[:, :, :, I_A:I_A + N], inner_s[:, :, :, I_A:I_A + N], ACT.Exp).then_inc(s_ca, 1)
                b = (0, 0)
                squares(xn[0][:, :, :], sq_a, a_cen, 1, a_sq)
                rstd(a_ps[0:CH, 1, 0:T], rstd_a, a_var, 1, a_ln, 1, a_rstd)
                xz_copy(b, 0, 0, 6)
                silu(b, 0)
                xproj_copy(b, 0)
                softplus(b, 0)
                for blk in range(4):
                    bc_copy(b, 0, blk)
                act.wait_ge(a_neg, 1)
                exps(b, 0, 0, NH)

            def finish(f):
                for gap in range(2 * GAPS):
                    fine(f, gap, True)

            program(step, act.Fori, front, finish)

        @block.vector
        def _(dve):
            def scan_step(b, q, phase):
                d, u, half = q // 6, (q // 2) % IC, q % 2
                x, dec = hs[half], decay[half]
                if phase == 0:
                    dve.wait_ge(dtu_ready, at(b, 2, d + 1))
                    dve.wait_ge(bc_copied, at(b, 64, 32 * d + 16 * half + 8))
                    wait(dve, ysum, at(b, SCANS, q - 1))
                    dve.tensor_tensor(x[:, :, :], states[half][:, :, :],
                                      dtu[d][:, u, :].unsqueeze(1).broadcast_to([128, NH, T]),
                                      ALU.mult).then_inc(dbu_done, 1)
                    if u == 0:
                        wait(dve, scan_done, at(b, SCANS, q - 1))
                        t = 0 if d == 0 else T - 1
                        dve.memset(dec[:, :, t:t + 1], 0.0).then_inc(edge, 1)
                if phase == 1:
                    dve.wait_ge(exp_done, at(b, SCANS, q + 1))
                    dve.wait_ge(dbu_done, at(b, SCANS, q + 1))
                    if u == 0:
                        dve.wait_ge(edge, at(b, 4, 2 * d + half + 1))
                    a = dec[:, :, :].rearrange("p n t -> p (n t)")
                    i = x[:, :, :].rearrange("p n t -> p (n t)")
                    if d == 1:
                        a, i = a[:, ::-1], i[:, ::-1]
                    dve.tensor_tensor_scan(i, a, i, 0.0, ALU.mult, ALU.add).then_inc(scan_done, 1)
                if phase == 2:
                    dve.wait_ge(scan_done, at(b, SCANS, q + 1))
                    dve.wait_ge(bc_copied, at(b, 64, 32 * d + 16 * half + 16))
                    dve.tensor_tensor(x[:, :, :], x[:, :, :], reads[half][:, :, :], ALU.mult).then_inc(hc_done, 1)

            def gate_unit(b, u):
                d, j = u // IC, u % IC
                dve.wait_ge(ysum, at(b, SCANS, 2 * u + 2))
                if u == 0:
                    wait(dve, out_mm, at(b, 1, 0))
                dve.scalar_tensor_tensor(out=yg[:, u, :], in0=xc[d][:, j, :], scalar=inner_s[:, d, j, I_D:I_D + 1],
                                         in1=y_ps[:, 0:T], op0=ALU.mult, op1=ALU.add).then_inc(gate_tmp, 1)
                dve.wait_ge(gate_tmp, at(b, UNITS, u + 1))
                dve.tensor_tensor(yg[:, u, :], yg[:, u, :], zs[d][:, j, :], ALU.mult).then_inc(gated, 1)

            def centre(x, out, bank, ready, value, done):
                dve.wait_ge(ready, value)
                dve.tensor_tensor(out[:, :, :], x[:, :, :], bank.unsqueeze(1).broadcast_to([CH, 2, T]),
                                  ALU.subtract).then_inc(done, 1)

            def scale_by(x, r, ready, value, done):
                dve.wait_ge(ready, value)
                dve.tensor_tensor(x[:, :, :], x[:, :, :], r[:, :].unsqueeze(1).broadcast_to([CH, 2, T]),
                                  ALU.mult).then_inc(done, 1)

            def affine(f, j, small):
                g = (P_N1LG, P_N1SG, P_N2LG, P_N2SG)[2 * j + small]
                dve.wait_ge(f_y, at(f, 4, 3 + j))
                for i in range(2):
                    a = dve.tensor_scalar(cen[:, i, :], cen[:, i, :], feat_s[:, i, g:g + 1],
                                          feat_s[:, i, g + 1:g + 2], ALU.mult, ALU.add)
                a.then_inc(f_aff, 1)

            def tok_add(b):
                dve.wait_ge(tok_mm, at(b, 1, 1))
                dve.scalar_tensor_tensor(
                    out=h[parity(b)][:, :, 1:1 + PATCHES],
                    in0=a_ps[0:CH, 0, 0:2 * PATCHES].rearrange("p (a t) -> p a t", a=2), scalar=1.0 / 255.0,
                    in1=feat_s[:, :, P_POS + 1:P_POS + 1 + PATCHES], op0=ALU.mult, op1=ALU.add)\
                    .then_inc(h_ready, 1)

            def conv(b, d, taps):
                for k in taps:
                    for j in range(IC):
                        n = 12 * d + 3 * k + j
                        t = k if d == 0 else 2 * PAD - k
                        w = inner_s[:, d, j, k:k + 1]
                        if k == 0:
                            dve.wait_ge(xz_copied, at(b, 12, 6 * d + j + 1))
                            dve.tensor_scalar(xc[d][:, j, :], xi[:, j, t:t + T], w, inner_s[:, d, j, I_CB:I_CB + 1],
                                              ALU.mult, ALU.add).then_inc(conv_tap, 1)
                        else:
                            dve.wait_ge(conv_tap, at(b, 24, n - 2))
                            dve.scalar_tensor_tensor(out=xc[d][:, j, :], in0=xi[:, j, t:t + T], scalar=w,
                                                     in1=xc[d][:, j, :], op0=ALU.mult, op1=ALU.add)\
                                .then_inc(conv_tap, 1)

            def split_parts(b, d):
                dve.wait_ge(xp_hi, at(b, 2, d + 1))
                rest = dt[d][:, 0, :]
                dve.tensor_tensor(rest[64:128, :], a_ps[64:128, 0, 0:T], parts[64:128, :], ALU.subtract)\
                    .then_inc(split, 1)
                dve.wait_ge(split, at(b, 6, 3 * d + 1))
                dve.tensor_copy(parts[64:128, :], rest[64:128, :]).then_inc(split, 1)
                dve.wait_ge(split, at(b, 6, 3 * d + 2))
                dve.tensor_tensor(parts[96:128, :], rest[96:128, :], parts[96:128, :], ALU.subtract)\
                    .then_inc(split, 1)

            def dt_max(b, d):
                for j in range(IC):
                    dve.wait_ge(dtv_abs, at(b, 6, 3 * d + j + 1))
                    if j == 0:
                        dve.wait_ge(split, at(b, 6, 3 * d + 3))
                    dve.tensor_scalar(dt[d][:, j, :], a_ps[:, (j + 1) % 2, 0:T], 0.0, None, ALU.max)\
                        .then_inc(dtv_max, 1)

            def dt_sum(b, d):
                dve.wait_ge(sp_ln, at(b, 2, d + 1))
                dve.wait_ge(dtv_max, at(b, 6, 3 * d + 3))
                dve.tensor_tensor(dt[d][:, :, :], dt[d][:, :, :], dtu[d][:, :, :], ALU.add).then_inc(dt_ready, 2)
                dve.wait_ge(dt_ready, at(b, 4, 2 * d + 2))
                dve.wait_ge(silu_done, at(b, 4, 2 * d + 2))
                dve.tensor_tensor(dtu[d][:, :, :], dt[d][:, :, :], xc[d][:, :, :], ALU.mult).then_inc(dtu_ready, 1)

            def residual(f):
                dve.wait_ge(out_mm, at(f, 1, 1))
                dve.tensor_tensor(res[:, :, :], f_ps[0:CH, 0:2, 0:T], xn[parity(f)][:, :, :], ALU.add)\
                    .then_inc(r_ready, 1)

            def add_mixer(f):
                dve.wait_ge(f_y, at(f, 4, 1))
                wait(dve, out_stored, at(f, 16, 0))
                for i in range(2):
                    dve.scalar_tensor_tensor(out=h2[:, i, :], in0=cen[:, i, :],
                                             scalar=feat_s[:, i, P_LNG:P_LNG + 1], in1=h[parity(f)][:, i, :],
                                             op0=ALU.mult, op1=ALU.add).then_inc(h2_tmp, 1)
                dve.wait_ge(h2_tmp, at(f, 2, 2))
                for i in range(2):
                    a = dve.tensor_scalar(h2[:, i, :], h2[:, i, :], feat_s[:, i, P_LNB:P_LNB + 1], None, ALU.add)
                a.then_inc(h2_ready, 1)

            def row_maxima(f, hd):
                s = hd % 2
                dve.wait_ge(sc_mm, at(f, HEADS, hd + 1))
                dve.tensor_reduce(row_max[:, s, :], f_ps[0:QT, 0:3, 0:T], AX_X, ALU.max).then_inc(mx_done, 1)
                dve.wait_ge(mx_done, at(f, HEADS, hd + 1))
                dve.tensor_scalar(neg_max[:, s, :], row_max[:, s, :], -HD ** -0.5, None, ALU.mult)\
                    .then_inc(nmx_done, 1)

            def normalise(f, hd):
                s = hd % 2
                dve.wait_ge(pexp, at(f, HEADS, hd + 1))
                dve.reciprocal(row_inv[:, s, :], row_sum[:, s, :]).then_inc(inv_done, 1)
                dve.wait_ge(inv_done, at(f, HEADS, hd + 1))
                for t in range(3):
                    a = dve.tensor_scalar(prob[s][:, t, :], prob[s][:, t, :], row_inv[:, s, t:t + 1], None, ALU.mult)
                a.then_inc(p_norm, 1)

            def add_gated(bank, i, g, step_sem):
                dve.scalar_tensor_tensor(out=res[:, i, :], in0=f_ps[0:CH, bank, 0:T], scalar=gate[:, g:g + 1],
                                         in1=res[:, i, :], op0=ALU.mult, op1=ALU.add).then_inc(step_sem, 1)

            def add_attention(f, small):
                dve.wait_ge(pr_mm, at(f, 1, 1))
                start = uneven(f, small, 2, 6, 0)
                for i in range(2):
                    if small:
                        add_gated(i, i, 0, x3_step)
                    else:
                        dve.scalar_tensor_tensor(out=res[:, i, :], in0=f_ps[0:CH, i, 0:T],
                                                 scalar=feat_s[:, i, P_BPROJ:P_BPROJ + 1], in1=res[:, i, :],
                                                 op0=ALU.add, op1=ALU.add).then_inc(x3_step, 1)
                if small:
                    dve.wait_ge(x3_step, start + 1)
                    add_gated(2, 0, 1, x3_step)
                    dve.wait_ge(x3_step, start + 3)
                    add_gated(3, 0, 2, x3_step)
                    dve.wait_ge(x3_step, start + 4)
                    for i in range(2):
                        dve.tensor_scalar(res[:, i, :], res[:, i, :], bias_sum[:, i, 0:1], None, ALU.add)\
                            .then_inc(x3_step, 1)

            def mlp_add_first(f):
                dve.wait_ge(fc2_mm, mlp_at(f, True, HC))
                add_gated(3, 0, 0, fin_step)
                add_gated(4, 1, 0, fin_step)

            def last_sum(f, small):
                start = uneven(f, small, 2, 6, 0)
                if small:
                    dve.wait_ge(fc2_mm, mlp_at(f, True, 2 * HC))
                    dve.wait_ge(fin_step, start + 2)
                    add_gated(2, 0, 1, fin_step)
                    dve.wait_ge(fc2_mm, mlp_at(f, True, 3 * HC))
                    dve.wait_ge(fin_step, start + 3)
                    add_gated(3, 0, 2, fin_step)
                    dve.wait_ge(fin_step, start + 4)
                    for i in range(2):
                        dve.tensor_scalar(res[:, i, :], res[:, i, :], bias_sum[:, i, 1:2], None, ALU.add)\
                            .then_inc(fin_step, 1)
                    dve.wait_ge(fin_step, start + 6)
                else:
                    dve.wait_ge(fc2_mm, mlp_at(f, False, HC))
                    for i in range(2):
                        dve.scalar_tensor_tensor(out=res[:, i, :], in0=f_ps[0:CH, 3 + i, 0:T],
                                                 scalar=feat_s[:, i, P_BFC2:P_BFC2 + 1], in1=res[:, i, :],
                                                 op0=ALU.add, op1=ALU.add).then_inc(fin_step, 1)
                    dve.wait_ge(fin_step, start + 2)
                dve.tensor_tensor(h2[:, :, :], h2[:, :, :], res[:, :, :], ALU.add).then_inc(out_ready, 1)

            def fine(f, gap, small):
                if gap == 5:
                    residual(f)
                if gap in (6, 8, 10, 29):
                    j = (6, 8, 10, 29).index(gap)
                    centre((res, h2, res, res)[j], (cen, res, cen, cen)[j], f_ps[0:CH, 2, 0:T],
                           f_mean, at(f, 4, j + 1), f_cen)
                if gap in (7, 9, 11, 30):
                    j = (7, 9, 11, 30).index(gap)
                    scale_by((cen, res, cen, cen)[j], rstd_f, f_rstd, at(f, 4, j + 1), f_y)
                    if j == 0:
                        add_mixer(f)
                    if j >= 2:
                        affine(f, j - 2, small)
                if 14 <= gap < 14 + HEADS:
                    row_maxima(f, gap - 14)
                if 15 <= gap < 15 + HEADS:
                    normalise(f, gap - 15)
                if gap == 28:
                    add_attention(f, small)
                if gap == 33 and small:
                    mlp_add_first(f)
                if gap == 35:
                    last_sum(f, small)

            def fronts(b, d, a, gap):
                x, xd = (b, 1) if d == 0 else (a, 0)
                if x is not None:
                    if gap == 3:
                        conv(x, xd, (0, 1))
                    if gap == 4:
                        conv(x, xd, (2, 3))
                    if gap == 8:
                        split_parts(x, xd)
                    if gap == 9:
                        dt_max(x, xd)
                    if gap == 10:
                        dt_sum(x, xd)
                if d == 0 and a is not None:
                    if gap == 10:
                        tok_add(a)
                    if gap == 11:
                        centre(h[parity(a)], xn[parity(a)], a_ps[0:CH, 1, 0:T], a_mean, at(a, 1, 1), a_cen)
                    if gap == 13:
                        scale_by(xn[parity(a)], rstd_a, a_rstd, at(a, 1, 1), xn_ready)

            def step(b, f, a, small):
                for d in range(2):
                    for gap in range(GAPS):
                        q = d * 6 + gap // 3
                        if gap % 6 == 3:
                            if q // 2 >= 1:
                                gate_unit(b, q // 2 - 1)
                            elif not first(b):
                                gate_unit(ago(b, 1), UNITS - 1)
                        scan_step(b, q, gap % 3)
                        if f is not None:
                            fine(f, d * GAPS + gap, small)
                        fronts(b, d, a, gap)

            def front():
                dve.memset(mean_w[:, :], 1.0 / C).then_inc(s_c, 1)
                dve.memset(eps_c[:, :], EPS).then_inc(s_c, 1)
                dve.memset(one_c[:, :], 1.0).then_inc(s_c, 1)
                dve.memset(xi[:, :, :], 0.0).then_inc(s_c, 1)
                dve.memset(dt_lo[:, :], 1.0).then_inc(s_c, 1)
                dve.wait_ge(s_w, 16 * len(LOADS))
                for i in range(2):
                    for c in range(2):
                        dve.tensor_tensor(h[c][:, i, 0:1], feat_s[:, i, P_CLS:P_CLS + 1],
                                          feat_s[:, i, P_POS:P_POS + 1], ALU.add).then_inc(s_c, 1)
                    dve.tensor_scalar(feat_s[:, i, P_POS + 1:FEAT_W], feat_s[:, i, P_POS + 1:FEAT_W],
                                      feat_s[:, i, P_TOKB:P_TOKB + 1], None, ALU.add).then_inc(s_c, 1)
                dve.memset(gate[2 * C // 6:CH, 2:3], 0.0).then_inc(s_c, 1)
                dve.wait_ge(s_c, 12)
                dve.tensor_reduce(gate_sum[:, 0:1], gate[:, 0:3], AX_X, ALU.add).then_inc(s_c, 1)
                dve.tensor_copy(gate_sum[:, 1:2], gate[:, 0:1]).then_inc(s_c, 1)
                dve.wait_ge(s_c, 14)
                for i in range(2):
                    for j, p in enumerate((P_BPROJ, P_BFC2)):
                        dve.tensor_tensor(bias_sum[:, i, j:j + 1], feat_s[:, i, p:p + 1], gate_sum[:, i:i + 1],
                                          ALU.mult).then_inc(s_c, 1)
                dve.wait_ge(s_c, CONSTS)
                b = (0, 0)
                tok_add(b)
                centre(h[0], xn[0], a_ps[0:CH, 1, 0:T], a_mean, 1, a_cen)
                dve.wait_ge(s_ca, 1)
                dve.tensor_scalar(inner_s[:, :, :, I_A:I_A + N], inner_s[:, :, :, I_A:I_A + N], -1.0, None,
                                  ALU.mult).then_inc(a_neg, 1)
                scale_by(xn[0], rstd_a, a_rstd, 1, xn_ready)
                conv(b, 0, range(TAPS))
                split_parts(b, 0)
                dt_max(b, 0)
                dt_sum(b, 0)

            def finish(f):
                gate_unit(f, UNITS - 1)
                for gap in range(2 * GAPS):
                    fine(f, gap, True)

            program(step, dve.Fori, front, finish)


def kernel(**inputs):
    import numpy as np
    import concourse.bacc as bacc
    from concourse.bass_utils import run_bass_kernel_spmd as run

    a = {k: np.asarray(v) for k, v in inputs.items()}

    def halves(w):
        return w.reshape(2, CH, *w.shape[1:]).swapaxes(0, 1)

    def chunks(w):
        return w.reshape(-1, 128, *w.shape[1:]).swapaxes(0, 1)

    def both(f):
        return np.stack([f("L0_attn_f_"), f("L0_attn_b_")], axis=1)

    def x_proj(p):
        w = a[p + "xp"].T
        wide = np.zeros((INNER, 128), w.dtype)
        wide[:, :RANK] = w[:, :RANK]
        for q in (32, 64, 96):
            wide[:, q:q + 2 * N] = w[:, RANK:]
        return chunks(wide)

    def inner(p):
        return chunks(np.concatenate([a[p + "cw"].T, a[p + "cb"][:, None], a[p + "D"][:, None], a[p + "Alog"]], 1))

    def spaced(w):
        wide = np.zeros((*w.shape[:-1], HEADS, 2 * HD), w.dtype)
        wide[..., :HD] = w.reshape(*w.shape[:-1], HEADS, HD)
        return wide.reshape(*w.shape[:-1], HEADS * 2 * HD)

    ff = "L0_ffn_"
    x = a["x"].reshape(BATCH, 14, 16, 14, 48).transpose(0, 2, 4, 1, 3)
    w_qkv = a[ff + "w_qkv"]
    vectors = [a["L0_tok_b"], a["L0_tok_class_token"], a["L0_attn_ln_g"], a["L0_attn_ln_b"]]
    vectors += [a[ff + n] for n in ("n1l_g", "n1l_b", "n1s_g", "n1s_b", "n2l_g", "n2l_b", "n2s_g", "n2s_b",
                                    "b_proj", "b_fc2")]
    arrays = {
        "patches": x.reshape(BATCH, KP, 128, PATCHES).transpose(0, 2, 1, 3),
        "txt": a["txt"].transpose(0, 2, 1).reshape(BATCH, 2, CH, TXT).transpose(0, 2, 1, 3),
        "tok_w": chunks(a["L0_tok_W"]),
        "feat": halves(np.concatenate([np.stack(vectors, 1), a["L0_tok_pos_emb"].T], 1)),
        "w_in": halves(both(lambda p: a[p + "in"].T)),
        "inner": both(inner),
        "x_proj": both(x_proj),
        "dt_w": both(lambda p: np.concatenate([a[p + "dtw"].T, a[p + "dtb"][None]], 0)),
        "w_out": both(lambda p: chunks(a[p + "out"].T)),
        "w_qk": halves(np.stack([spaced(w_qkv[:, :C]), spaced(w_qkv[:, C:2 * C])], 1)),
        "w_v": halves(np.pad(w_qkv[:, 2 * C:], ((0, 0), (0, HD)))),
        "w_proj": chunks(spaced(a[ff + "w_proj"].T).T),
        "fc1": halves(a[ff + "w_fc1"]),
        "fc1_b": chunks(a[ff + "b_fc1"]),
        "fc2": chunks(a[ff + "w_fc2"]),
        "gumbel": np.broadcast_to(a[ff + "gumbel_weights"], (CH, 3)),
    }
    arrays = {k: np.ascontiguousarray(v) for k, v in arrays.items()}
    nc = bacc.Bacc("TRN2", target_bir_lowering=False, num_devices=1)
    args = {k: nc.dram_tensor(f"in_{k}", v.shape, mybir.dt.from_np(v.dtype), kind="ExternalInput").ap()
            for k, v in arrays.items()}
    out = nc.dram_tensor("out_0", (BATCH, CH, 2, T), F32, kind="ExternalOutput").ap()
    build(nc, **args, out=out)
    r = run(nc, [{f"in_{k}": v for k, v in arrays.items()}], core_ids=[0])
    got = r.results[0]["out_0"]
    return np.ascontiguousarray(got.transpose(0, 3, 2, 1).reshape(BATCH, T, C))
```

```python
from contextlib import ExitStack

import concourse.bass as bass
from concourse import mybir

F32 = mybir.dt.float32
BF16 = mybir.dt.bfloat16
ALU = mybir.AluOpType
ACT = mybir.ActivationFunctionType
AX_X = mybir.AxisListType.X

BATCH = 32
LARGE = BATCH // 2
PATCHES = 196
PD = 768
KP = PD // 128
TXT = 77
T = 1 + PATCHES + TXT
C = 192
CH = C // 2
INNER = 384
IC = INNER // 128
N = 16
NH = N // 2
RANK = 12
TAPS = 4
PAD = TAPS - 1
XI_W = T + 2 * PAD
UNITS = 2 * IC
SCANS = 2 * UNITS
HEADS = 12
HD = C // HEADS
GROUPS = HEADS // 4
QS = (0, 91, 182)
QT = 92
HID = 4 * C
HC = HID // 128
EPS = 1e-5
GAPS = 18

(P_TOKB, P_CLS, P_LNG, P_LNB, P_N1LG, P_N1LB, P_N1SG, P_N1SB, P_N2LG, P_N2LB, P_N2SG, P_N2SB,
 P_BPROJ, P_BFC2) = range(14)
P_POS = 14
FEAT_W = P_POS + 1 + PATCHES
I_CB, I_D, I_A = TAPS, TAPS + 1, TAPS + 2
INNER_W = I_A + N


def ago(b, m):
    return (b[0], b[1] - m)


def parity(b):
    return b[1] % 2


def first(b):
    return isinstance(b[0], int) and b[1] == 0


def last(b):
    return isinstance(b[0], int) and b[1] == BATCH - 1


def number(b):
    return b[0] * 2 + b[1]


def at(b, per_batch, n):
    return b[0] * (2 * per_batch) + (b[1] * per_batch + n)


def uneven(b, small, per_large, per_small, n):
    if not small:
        return at(b, per_large, n)
    return at(b, per_small, n - LARGE * (per_small - per_large))


def mlp_at(b, small, n):
    return uneven(b, small, HC, 3 * HC, n)


def variant_at(b, small, n):
    return uneven(b, small, 1, 3, n)


def every_other(b, n):
    return b[0] * n + (b[1] // 2 + 1) * n


def wait(eng, sem, value):
    if isinstance(value, int) and value <= 0:
        return
    eng.wait_ge(sem, value)


def build(nc, patches, txt, tok_w, feat, w_in, inner, x_proj, dt_w, w_out, w_qk, w_v, w_proj,
          fc1, fc1_b, fc2, gumbel, out):
    with ExitStack() as ctx:
        def sb(name, shape, dt=F32):
            return ctx.enter_context(nc.sbuf_tensor(name, shape, dt))

        def sem(name):
            return ctx.enter_context(nc.semaphore(name))

        tok_w_s = sb("tok_w_s", [128, KP, C])
        feat_s = sb("feat_s", [CH, 2, FEAT_W])
        w_in_s = sb("w_in_s", [CH, 2, 2, 2 * INNER])
        inner_s = sb("inner_s", [128, 2, IC, INNER_W])
        x_proj_s = sb("x_proj_s", [128, 2, IC, 128])
        dt_w_s = sb("dt_w_s", [RANK + 1, 2, INNER])
        w_out_s = sb("w_out_s", [128, 2, IC, C])
        w_qk_s = sb("w_qk_s", [CH, 2, 2, GROUPS * 128])
        w_v_s = sb("w_v_s", [CH, 2, C + HD])
        w_proj_s = sb("w_proj_s", [128, GROUPS, C])
        fc1_s = sb("fc1_s", [CH, 2, HID])
        fc1_b_s = sb("fc1_b_s", [128, HC])
        fc2_s = sb("fc2_s", [128, HC, C])
        gate = sb("gate", [CH, 3])
        bias_sum = sb("bias_sum", [CH, 2, 2])
        gate_sum = sb("gate_sum", [CH, 2])
        ident = sb("ident", [128, 128])
        mean_w = sb("mean_w", [CH, CH])
        pick = sb("pick", [128, 32], BF16)
        v_mask = sb("v_mask", [QT, 3])
        eps_c = sb("eps_c", [128, 1])
        one_c = sb("one_c", [128, 1])

        xp = sb("xp", [128, KP, PATCHES])
        h = [sb(f"h{i}", [CH, 2, T]) for i in range(2)]
        xn = [sb(f"xn{i}", [CH, 2, T]) for i in range(2)]
        h2 = sb("h2", [CH, 2, T])
        res = sb("res", [CH, 2, T])
        cen = sb("cen", [CH, 2, T])
        rstd_a = sb("rstd_a", [CH, T])
        rstd_f = sb("rstd_f", [CH, T])
        xi = sb("xi", [128, IC, XI_W])
        zs = [sb(f"zs{d}", [128, IC, T]) for d in range(2)]
        xc = [sb(f"xc{d}", [128, IC, T]) for d in range(2)]
        dt = [sb(f"dt{d}", [128, IC, T]) for d in range(2)]
        dtu = [sb(f"dtu{d}", [128, IC, T]) for d in range(2)]
        parts = sb("parts", [128, T], BF16)
        dt_lo = sb("dt_lo", [RANK + 1, T])
        states = [sb(f"b_rows{i}", [128, NH, T]) for i in range(2)]
        reads = [sb(f"c_rows{i}", [128, NH, T]) for i in range(2)]
        decay = [sb(f"decay{i}", [128, NH, T]) for i in range(2)]
        hs = [sb(f"hs{i}", [128, NH, T]) for i in range(2)]
        yg = sb("yg", [128, UNITS, T])
        qk = sb("qk", [128, 2, T])
        v_s = sb("v_s", [QT, 3, C + HD])
        hid = sb("hid", [128, 3 * HC, T])
        prob_t = hid[0:QT, 0:12, :].rearrange("p (r k) t -> p r k t", r=4)
        prob = [hid[0:QT, 12 + 3 * i:15 + 3 * i, :] for i in range(2)]
        neg_max = sb("neg_max", [QT, 2, 3])
        row_max = sb("row_max", [QT, 2, 3])
        row_sum = sb("row_sum", [QT, 2, 3])
        row_inv = sb("row_inv", [QT, 2, 3])
        o_s = sb("o_s", [128, GROUPS, T])
        sq_a = xp[0:CH, 0:3, :].rearrange("p a t -> p (a t)")[:, 0:2 * T].rearrange("p (a t) -> p a t", a=2)
        sq_f = hid[0:CH, 0:2, :]

        y_ps = ctx.enter_context(nc.psum_tensor("y_ps", [128, 512], F32))
        a_ps = ctx.enter_context(nc.psum_tensor("a_ps", [128, 2, 512], F32))
        f_ps = ctx.enter_context(nc.psum_tensor("f_ps", [128, 5, 512], F32))

        s_w = sem("weights_loaded")
        s_c = sem("constants_made")
        s_cp = sem("constants_pool")
        s_ca = sem("constants_act")
        s_x = sem("patches_loaded")
        s_txt = [sem(f"txt_loaded{i}") for i in range(2)]
        tok_mm = sem("tok_mm")
        h_ready = sem("h_ready")
        a_mean = sem("a_mean")
        a_cen = sem("a_cen")
        a_sq = sem("a_sq")
        a_var = sem("a_var")
        a_ln = sem("a_ln")
        a_rstd = sem("a_rstd")
        xn_ready = sem("xn_ready")
        xz_mm = sem("xz_mm")
        xz_copied = sem("xz_copied")
        conv_tap = sem("conv_tap")
        silu_done = sem("silu_done")
        xp_mm = sem("xproj_mm")
        xp_hi = sem("xproj_hi")
        dtlo_ready = sem("dtlo_ready")
        split = sem("split")
        dtv_mm = sem("dtv_mm")
        dtv_abs = sem("dtv_abs")
        dtv_max = sem("dtv_max")
        sp_exp = sem("softplus_exp")
        sp_ln = sem("softplus_ln")
        dt_ready = sem("dt_ready")
        dtu_ready = sem("dtu_ready")
        bc_mm = sem("bc_mm")
        bc_copied = sem("bc_copied")
        a_neg = sem("a_negated")
        edge = sem("edge_zeroed")
        exp_done = sem("exp_done")
        dbu_done = sem("dbu_done")
        scan_done = sem("scan_done")
        hc_done = sem("hc_done")
        ysum = sem("ysum")
        gate_tmp = sem("gate_tmp")
        gated = sem("gated")
        out_mm = sem("out_mm")
        r_ready = sem("r_ready")
        f_mean = sem("f_mean")
        f_cen = sem("f_cen")
        f_sq = sem("f_sq")
        f_var = sem("f_var")
        f_ln = sem("f_ln")
        f_rstd = sem("f_rstd")
        f_y = sem("f_y")
        f_aff = sem("f_affine")
        h2_tmp = sem("h2_tmp")
        h2_ready = sem("h2_ready")
        qk_mm = sem("qk_mm")
        qk_copied = sem("qk_copied")
        v_mm = sem("v_mm")
        v_copied = sem("v_copied")
        sc_mm = sem("scores_mm")
        mx_done = sem("mx_done")
        nmx_done = sem("nmx_done")
        pexp = sem("prob_exp")
        inv_done = sem("inv_done")
        p_norm = sem("prob_normed")
        pt_mm = sem("prob_t_mm")
        pt_copied = sem("prob_t_copied")
        av_mm = sem("av_mm")
        av_copied = sem("av_copied")
        pr_mm = sem("proj_mm")
        x3_step = sem("x3_step")
        fc1_mm = sem("fc1_mm")
        fc1_copied = sem("fc1_copied")
        gelu_done = sem("gelu_done")
        fc2_mm = sem("fc2_mm")
        mlp_added = sem("mlp_added")
        fin_step = sem("fin_step")
        out_ready = sem("out_ready")
        out_stored = sem("out_stored")

        LOADS = [(tok_w_s, tok_w), (feat_s, feat), (w_in_s, w_in), (inner_s, inner), (x_proj_s, x_proj),
                 (dt_w_s, dt_w), (w_out_s, w_out), (w_qk_s, w_qk), (w_v_s, w_v), (w_proj_s, w_proj),
                 (fc1_s, fc1), (fc1_b_s, fc1_b), (fc2_s, fc2), (gate, gumbel)]
        CONSTS = 18
        ROWS = {gap: (4 * i, 4 * i + 4) for i, gap in enumerate((13, 14, 15, 16, 17, 0, 1, 2))}
        EARLY_ROWS = 20

        VAR_GAPS = (7, 9, 11, 34)
        QK_GAPS = (12, 18, 23)
        SCORE_GAPS = [14 + hd + hd // 4 for hd in range(HEADS)]
        TURN_GAPS = [gap + 2 for gap in SCORE_GAPS]
        AV_GAPS = (20, 25, 30)
        VARIANTS = [(CH, 2, (3, 4)), (CH, 1, (2,)), (C // 3, 1, (0,))]

        block = ctx.enter_context(nc.Block())

        def bc_rows(b, d, a, gap):
            if gap >= GAPS - 5:
                x, xd = (b, 1) if d == 0 else (a, 0)
            else:
                x, xd = (b, d)
                if first(b) and d == 0:
                    x = None
            if gap not in ROWS or x is None:
                return None
            return (x, xd, *ROWS[gap])

        def endings(d, gap, f, e):
            if d == 0 and gap <= 4 and e is not None:
                yield (*e, 2 * GAPS + gap)
            if f is not None:
                yield (*f, d * GAPS + gap)

        def program(step, gaps_loop, front, finish):
            front()
            step((0, 0), None, None, (0, 1))
            step((0, 1), ((0, 0), False), None, (0, 2))
            step((0, 2), ((0, 1), False), ((0, 0), False), (0, 3))
            with gaps_loop(1, LARGE // 2) as r:
                for off in (1, 2):
                    step((r, off), ((r, off - 1), False), ((r, off - 2), False), (r, off + 1))
            step((0, LARGE + 1), ((0, LARGE), True), ((0, LARGE - 1), False), (0, LARGE + 2))
            step((0, LARGE + 2), ((0, LARGE + 1), True), ((0, LARGE), True), (0, LARGE + 3))
            with gaps_loop(LARGE // 2 + 1, BATCH // 2 - 1) as r:
                for off in (1, 2):
                    step((r, off), ((r, off - 1), True), ((r, off - 2), True), (r, off + 1))
            step((0, BATCH - 1), ((0, BATCH - 2), True), ((0, BATCH - 3), True), None)
            finish(((0, BATCH - 1), True), ((0, BATCH - 2), True))

        @block.sync
        def _(sp):
            def load_patches(b):
                wait(sp, a_var, at(b, 1, 0))
                wait(sp, tok_mm, at(b, 1, 0))
                sp.dma_start(xp[:, :, :], patches[number(b)]).then_inc(s_x, 16)

            def load_txt(b):
                wait(sp, h2_ready, at(ago(b, 1), 1, 0))
                sp.dma_start(h[parity(b)][:, :, 1 + PATCHES:T], txt[number(b)]).then_inc(s_txt[parity(b)], 16)

            def store(b):
                sp.wait_ge(out_ready, at(b, 1, 1))
                sp.dma_start(out[number(b)], h2[:, :, :]).then_inc(out_stored, 16)

            def front():
                load_patches((0, 0))
                load_txt((0, 0))
                for dst, src in LOADS:
                    sp.dma_start(dst[tuple(slice(None) for _ in dst.shape)], src).then_inc(s_w, 16)

            def step(b, f, e, a):
                if a is not None:
                    load_patches(a)
                if e is not None:
                    store(e[0])
                if a is not None:
                    load_txt(a)

            def finish(f, e):
                store(e[0])
                store(f[0])
                sp.wait_ge(out_stored, at(f[0], 16, 16))

            program(step, sp.Fori, front, finish)

        @block.gpsimd
        def _(pool):
            pool.memset(ident[:, :], 0.0).then_inc(s_cp, 1)
            pool.memset(pick[:, :], 0.0).then_inc(s_cp, 1)
            pool.memset(v_mask[:, :], 1.0).then_inc(s_cp, 1)
            pool.wait_ge(s_cp, 3)
            pool.affine_select(out=ident[:, :], in_=ident[:, :], compare_op=ALU.not_equal, fill=1.0, base=0,
                               pattern=[[-1, 128]], channel_multiplier=1).then_inc(s_cp, 1)
            for q in (1, 2, 3):
                pool.affine_select(out=pick[:, :], in_=pick[:, :], compare_op=ALU.not_equal, fill=1.0,
                                   base=-32 * q, pattern=[[-1, 32]], channel_multiplier=1).then_inc(s_cp, 1)
                pool.wait_ge(s_cp, 4 + q)
            pool.memset(v_mask[0:1, 1:3], 0.0).then_inc(s_cp, 1)

        @block.tensor
        def _(pe):
            def mean_mm(bank, x, done):
                for i in range(2):
                    mm = pe.matmul(bank[0:CH, 0:T], mean_w[:, :], x[:, i, :], start=(i == 0), stop=(i == 1))
                mm.then_inc(done, 1)

            def ysum_part(b, q, lo, hi, between=None):
                if lo == 0:
                    wait(pe, hc_done, at(b, SCANS, q + 1))
                    if q % 2 == 0:
                        wait(pe, gate_tmp, at(b, UNITS, q // 2))
                for n in range(lo, hi):
                    if between:
                        between()
                    mm = pe.matmul(y_ps[:, 0:T], ident[:, :], hs[q % 2][:, n, :],
                                   start=(q % 2 == 0 and n == 0), stop=(q % 2 == 1 and n == NH - 1))
                    if n == NH - 1:
                        mm.then_inc(ysum, 1)

            def tok(b):
                pe.wait_ge(s_x, at(b, 16, 16))
                wait(pe, dtv_abs, at(b, 6, -1))
                wait(pe, dtv_max, at(b, 6, -1))
                for i in range(2):
                    for k in range(KP):
                        mm = pe.matmul(a_ps[0:CH, 0, i * PATCHES:(i + 1) * PATCHES],
                                       tok_w_s[:, k, i * CH:(i + 1) * CH], xp[:, k, :],
                                       start=(k == 0), stop=(k == KP - 1))
                mm.then_inc(tok_mm, 1)

            def a_mean_mm(b):
                pe.wait_ge(h_ready, at(b, 1, 1))
                pe.wait_ge(s_txt[parity(b)], every_other(b, 16))
                wait(pe, dtv_abs, at(b, 6, 0))
                wait(pe, dtv_max, at(b, 6, 0))
                mean_mm(a_ps[:, 1, :], h[parity(b)], a_mean)

            def a_var_mm(b):
                pe.wait_ge(a_sq, at(b, 1, 1))
                mean_mm(a_ps[:, 1, :], sq_a, a_var)

            def in_proj(b, d, lo, hi):
                if lo == 0:
                    pe.wait_ge(xn_ready, at(b, 1, 1))
                    wait(pe, bc_copied, at(b, 64, 32 * d))
                for j in range(lo, hi):
                    if j >= 2:
                        pe.wait_ge(xz_copied, at(b, 12, 6 * d + j - 1))
                    for i in range(2):
                        mm = pe.matmul(a_ps[:, j % 2, 0:T], w_in_s[:, i, d, j * 128:(j + 1) * 128],
                                       xn[parity(b)][:, i, :], start=(i == 0), stop=(i == 1))
                    mm.then_inc(xz_mm, 1)

            def x_proj_mm(b, d):
                pe.wait_ge(xz_copied, at(b, 12, 6 * d + 6))
                pe.wait_ge(silu_done, at(b, 4, 2 * d + 1))
                for k in range(IC):
                    mm = pe.matmul(a_ps[:, 0, 0:T], x_proj_s[:, d, k, :], xc[d][:, k, :],
                                   start=(k == 0), stop=(k == IC - 1))
                mm.then_inc(xp_mm, 1)

            def dt_mm(b, d, lo, hi):
                pe.wait_ge(dtlo_ready, at(b, 2, d + 1))
                for j in range(lo, hi):
                    bank = (j + 1) % 2
                    if j == 1:
                        pe.wait_ge(split, at(b, 6, 3 * d + 3))
                    if j == 2:
                        pe.wait_ge(dtv_abs, at(b, 6, 3 * d + 1))
                        pe.wait_ge(dtv_max, at(b, 6, 3 * d + 1))
                    pe.matmul(a_ps[:, bank, 0:T], dt_w_s[:, d, j * 128:(j + 1) * 128], dt_lo[:, :],
                              start=True, stop=True).then_inc(dtv_mm, 1)

            def bc_row(b, d, i):
                if i == 0:
                    pe.wait_ge(dtv_abs, at(b, 6, 3 * d + 3))
                    pe.wait_ge(dtv_max, at(b, 6, 3 * d + 3))
                    if d == 1 and not last(b):
                        pe.wait_ge(h_ready, at(b, 1, 2))
                if i == 1 and d == 1 and not last(b):
                    pe.wait_ge(a_ln, at(b, 1, 2))
                if i >= 2:
                    pe.wait_ge(bc_copied, at(b, 64, 32 * d + i - 1))
                kind, half, n = (i // 8) % 2, i // 16, i % 8
                row = N * kind + NH * half + n
                pe.matmul(a_ps[:, i % 2, 0:T], pick[:, row:row + 1].broadcast_to([128, 128]), parts[:, :],
                          start=True, stop=True).then_inc(bc_mm, 1)

            def out_proj(f):
                pe.wait_ge(gated, at(f, UNITS, UNITS))
                wait(pe, mlp_added, at(f, 2, 0))
                for i in range(2):
                    for u in range(UNITS):
                        mm = pe.matmul(f_ps[0:CH, 3 + i, 0:T], w_out_s[:, u // IC, u % IC, i * CH:(i + 1) * CH],
                                       yg[:, u, :], start=(u == 0), stop=(u == UNITS - 1))
                mm.then_inc(out_mm, 1)

            def f_mean_mm(f, j, x, ready, value):
                pe.wait_ge(ready, value)
                mean_mm(f_ps[:, 2, :], x, f_mean)

            def f_var_mm(f, j):
                pe.wait_ge(f_sq, at(f, 4, j + 1))
                mean_mm(f_ps[:, 3, :], sq_f, f_var)

            def qk_mms(f, g):
                if g == 0:
                    pe.wait_ge(f_aff, at(f, 2, 1))
                else:
                    pe.wait_ge(pexp, at(f, HEADS, 4 * g))
                for s in range(2):
                    for i in range(2):
                        mm = pe.matmul(f_ps[:, s, 0:T], w_qk_s[:, i, s, g * 128:(g + 1) * 128], cen[:, i, :],
                                       start=(i == 0), stop=(i == 1))
                    mm.then_inc(qk_mm, 1)

            def v_mms(f):
                for t in range(3):
                    for i in range(2):
                        mm = pe.matmul(f_ps[0:QT, 2 + t, 0:C + HD], cen[:, i, QS[t]:QS[t] + QT], w_v_s[:, i, :],
                                       start=(i == 0), stop=(i == 1))
                    mm.then_inc(v_mm, 1)

            def scores(f, hd):
                g, r = hd // 4, 32 * (hd % 4)
                pe.wait_ge(qk_copied, at(f, 2 * GROUPS, 2 * g + 2))
                if hd == 0:
                    pe.wait_ge(v_copied, at(f, 3, 3))
                else:
                    pe.wait_ge(pexp, at(f, HEADS, hd))
                for t in range(3):
                    mm = pe.matmul(f_ps[0:QT, t, 0:T], qk[r:r + HD, 0, QS[t]:QS[t] + QT], qk[r:r + HD, 1, :],
                                   start=True, stop=True)
                mm.then_inc(sc_mm, 1)

            def turn(f, hd, lo, hi):
                pe.wait_ge(p_norm, at(f, HEADS, hd + 1))
                for t in range(lo, hi):
                    n = 3 * hd + t
                    if n >= 2:
                        pe.wait_ge(pt_copied, at(f, 3 * HEADS, n - 1))
                    if n in (12, 24):
                        pe.wait_ge(av_copied, at(f, GROUPS, n // 12))
                    for k in range(3):
                        mm = pe.transpose(f_ps[0:QT, 3 + n % 2, k * QT:(k + 1) * QT],
                                          prob[hd % 2][:, t, QS[k]:QS[k] + QT], ident[0:QT, 0:QT])
                    mm.then_inc(pt_mm, 1)

            def av(f, g):
                pe.wait_ge(pt_copied, at(f, 3 * HEADS, 12 * g + 12))
                for k in range(3):
                    for r in range(4):
                        hd = 4 * g + r
                        mm = pe.matmul(f_ps[32 * r:32 * r + 32, 3, 0:T], v_s[:, k, hd * HD:hd * HD + 2 * HD],
                                       prob_t[:, r, k, :], start=(k == 0), stop=(k == 2),
                                       skip_group_check=True)
                mm.then_inc(av_mm, 1)

            def proj(f, small):
                pe.wait_ge(av_copied, at(f, GROUPS, GROUPS))
                for i in range(2):
                    for g in range(GROUPS):
                        mm = pe.matmul(f_ps[0:CH, i, 0:T], w_proj_s[:, g, i * CH:(i + 1) * CH], o_s[:, g, :],
                                       start=(g == 0), stop=(g == GROUPS - 1))
                if small:
                    pe.matmul(f_ps[0:CH, 2, 0:T], w_proj_s[:, 0, 0:CH], o_s[:, 0, :], start=True, stop=False)
                    pe.matmul(f_ps[0:CH, 2, 0:T], w_proj_s[0:64, 1, 0:CH], o_s[0:64, 1, :],
                              start=False, stop=True)
                    mm = pe.matmul(f_ps[0:CH, 3, 0:T], w_proj_s[:, 0, 0:CH], o_s[:, 0, :], start=True, stop=True)
                mm.then_inc(pr_mm, 1)

            def fc1_mms(f, small, variants):
                for q in range(HC * variants[0], HC * (variants[-1] + 1)):
                    if q == 0:
                        pe.wait_ge(f_aff, at(f, 2, 2))
                    if q >= 2:
                        pe.wait_ge(fc1_copied, mlp_at(f, small, q - 1))
                    rows, n = VARIANTS[q // HC][0:2]
                    ch = q % HC
                    for i in range(n):
                        mm = pe.matmul(f_ps[:, q % 2, 0:T], fc1_s[0:rows, i, ch * 128:(ch + 1) * 128],
                                       cen[0:rows, i, :], start=(i == 0), stop=(i == n - 1))
                    mm.then_inc(fc1_mm, 1)

            def fc2_mms(f, small, v):
                pe.wait_ge(gelu_done, variant_at(f, small, v + 1))
                for i, bank in enumerate(VARIANTS[v][2]):
                    for ch in range(HC):
                        mm = pe.matmul(f_ps[0:CH, bank, 0:T], fc2_s[:, ch, i * CH:(i + 1) * CH],
                                       hid[:, HC * v + ch, :], start=(ch == 0), stop=(ch == HC - 1))
                mm.then_inc(fc2_mm, 1)

            def fine_early(f, small, gap):
                if gap == 4:
                    out_proj(f)
                if gap == 6:
                    f_mean_mm(f, 0, res, r_ready, at(f, 1, 1))
                if gap in VAR_GAPS:
                    f_var_mm(f, VAR_GAPS.index(gap))
                if gap == 8:
                    f_mean_mm(f, 1, h2, h2_ready, at(f, 1, 1))
                if gap == 10:
                    f_mean_mm(f, 2, res, f_y, at(f, 4, 2))
                if gap == 13:
                    v_mms(f)
                if gap in QK_GAPS:
                    qk_mms(f, QK_GAPS.index(gap))
                if gap in SCORE_GAPS:
                    scores(f, SCORE_GAPS.index(gap))
                if gap in TURN_GAPS:
                    turn(f, TURN_GAPS.index(gap), 0, 2)
                if gap in AV_GAPS:
                    av(f, AV_GAPS.index(gap))
                if gap == 31:
                    proj(f, small)
                if gap == 33:
                    f_mean_mm(f, 3, res, x3_step, uneven(f, small, 2, 5, 5 if small else 2))

            def fine_late(f, small, gap):
                if gap in TURN_GAPS:
                    turn(f, TURN_GAPS.index(gap), 2, 3)
                if gap == 35:
                    fc1_mms(f, small, (0,))
                if gap == 36 and small:
                    fc1_mms(f, small, (1, 2))
                if gap == 37:
                    fc2_mms(f, small, 0)
                if gap == 38 and small:
                    fc2_mms(f, small, 1)
                    fc2_mms(f, small, 2)

            def fronts(b, d, a, gap):
                x, xd = (b, 1) if d == 0 else (a, 0)
                if x is not None:
                    if gap in (3, 4, 5):
                        in_proj(x, xd, 2 * gap - 6, 2 * gap - 4)
                    if gap == 7:
                        x_proj_mm(x, xd)
                    if gap == 9:
                        dt_mm(x, xd, 0, 2)
                    if gap == 10:
                        dt_mm(x, xd, 2, 3)

            def fronts_early(b, d, a, gap):
                if d == 0 and a is not None:
                    if gap == 11:
                        tok(a)
                    if gap == 12:
                        a_mean_mm(a)
                    if gap == 13:
                        a_var_mm(a)

            def step(b, f, e, a):
                for d in range(2):
                    for gap in range(GAPS):
                        fronts_early(b, d, a, gap)
                        for part in endings(d, gap, f, e):
                            fine_early(*part)
                        rows = bc_rows(b, d, a, gap)
                        todo = iter(range(rows[2], rows[3])) if rows else iter(())

                        def between():
                            i = next(todo, None)
                            if i is not None:
                                bc_row(rows[0], rows[1], i)

                        q = d * 6 + gap // 3 - 1
                        lo, hi = [(0, 3), (3, 6), (6, 8)][gap % 3]
                        if q >= 0:
                            ysum_part(b, q, lo, hi, between if gap != 13 else None)
                        elif not first(b):
                            ysum_part(ago(b, 1), SCANS - 1, lo, hi, between)
                        for i in todo:
                            bc_row(rows[0], rows[1], i)
                        for part in endings(d, gap, f, e):
                            fine_late(*part)
                        fronts(b, d, a, gap)

            def front():
                pe.wait_ge(s_w, 16 * len(LOADS))
                pe.wait_ge(s_cp, 8)
                pe.wait_ge(s_c, CONSTS)
                b = (0, 0)
                tok(b)
                a_mean_mm(b)
                a_var_mm(b)
                in_proj(b, 0, 0, 6)
                x_proj_mm(b, 0)
                dt_mm(b, 0, 0, IC)
                for i in range(32):
                    bc_row(b, 0, i)

            def finish(f, e):
                for gap in range(2 * GAPS + 5):
                    if gap <= 4:
                        fine_early(*e, 2 * GAPS + gap)
                        fine_late(*e, 2 * GAPS + gap)
                    if gap == 2:
                        ysum_part(f[0], SCANS - 1, 0, NH)
                    fine_early(*f, gap)
                    fine_late(*f, gap)

            program(step, pe.Fori, front, finish)

        @block.scalar
        def _(act):
            def exps(b, q, lo, hi):
                d, u, half = q // 6, (q // 2) % IC, q % 2
                if lo == 0:
                    act.wait_ge(dt_ready, at(b, 4, 2 * d + 2))
                    wait(act, scan_done, at(b, SCANS, q - 1))
                for n in range(lo, hi):
                    s = I_A + NH * half + n
                    t = slice(1, T) if d == 0 else slice(0, T - 1)
                    e = act.activation(decay[half][:, n, t], dt[d][:, u, t], ACT.Exp,
                                       scale=inner_s[:, d, u, s:s + 1])
                if hi == NH:
                    e.then_inc(exp_done, 1)

            def squares(x, out, ready, value, done):
                act.wait_ge(ready, value)
                act.activation(out, x, ACT.Square).then_inc(done, 1)

            def rstd(bank, out, ready, value, ln_sem, ln_value, done):
                act.wait_ge(ready, value)
                act.activation(out[:, :], bank, ACT.Ln, bias=eps_c[0:CH, 0:1]).then_inc(ln_sem, 1)
                act.wait_ge(ln_sem, ln_value)
                act.activation(out[:, :], out[:, :], ACT.Exp, scale=-0.5).then_inc(done, 1)

            def xz_copy(b, d, lo, hi):
                for j in range(lo, hi):
                    act.wait_ge(xz_mm, at(b, 12, 6 * d + j + 1))
                    if j == 0:
                        wait(act, conv_tap, at(b, 24, 12 * d))
                    if j == IC:
                        wait(act, gated, at(ago(b, 1), UNITS, IC * (d + 1)))
                    dst = xi[:, j, PAD:PAD + T] if j < IC else zs[d][:, j - IC, :]
                    act.activation(dst, a_ps[:, j % 2, 0:T], ACT.Copy).then_inc(xz_copied, 1)

            def silu(b, d):
                act.wait_ge(conv_tap, at(b, 24, 12 * d + 12))
                act.wait_ge(xz_copied, at(b, 12, 6 * d + 6))
                act.activation(xc[d][:, :, :], xc[d][:, :, :], ACT.Silu).then_inc(silu_done, 1)
                act.activation(zs[d][:, :, :], zs[d][:, :, :], ACT.Silu).then_inc(silu_done, 1)
                act.preload_act_table_set("natural_log_exp_and_others")

            def xproj_copy(b, d):
                act.wait_ge(xp_mm, at(b, 2, d + 1))
                wait(act, dtv_mm, at(b, 6, 3 * d))
                act.activation(dt_lo[0:RANK, :], a_ps[0:RANK, 0, 0:T], ACT.Copy).then_inc(dtlo_ready, 1)
                wait(act, bc_mm, at(b, 64, 32 * d))
                act.activation(parts[:, :], a_ps[:, 0, 0:T], ACT.Copy).then_inc(xp_hi, 1)

            def dt_abs(b, d, lo, hi):
                for j in range(lo, hi):
                    act.wait_ge(dtv_mm, at(b, 6, 3 * d + j + 1))
                    act.activation(dtu[d][:, j, :], a_ps[:, (j + 1) % 2, 0:T], ACT.Abs).then_inc(dtv_abs, 1)

            def softplus(b, d):
                act.wait_ge(dtv_abs, at(b, 6, 3 * d + 3))
                act.activation(dtu[d][:, :, :], dtu[d][:, :, :], ACT.Exp, scale=-1.0).then_inc(sp_exp, 1)
                act.wait_ge(sp_exp, at(b, 2, d + 1))
                act.activation(dtu[d][:, :, :], dtu[d][:, :, :], ACT.Ln, bias=one_c[:, 0:1]).then_inc(sp_ln, 1)

            def bc_copy(b, d, lo, hi):
                before, last_scan = (ago(b, 1), SCANS - 2) if d == 0 else (b, SCANS // 2 - 2)
                for i in range(lo, hi):
                    blk = i // 8
                    if i % 8 == 0:
                        wait(act, (dbu_done, hc_done)[blk % 2], at(before, SCANS, last_scan + 1 + blk // 2))
                    act.wait_ge(bc_mm, at(b, 64, 32 * d + i + 1))
                    act.activation((states, reads)[blk % 2][blk // 2][:, i % 8, :], a_ps[:, i % 2, 0:T],
                                   ACT.Copy).then_inc(bc_copied, 1)

            def qk_copy(f, g):
                for s in range(2):
                    act.wait_ge(qk_mm, at(f, 2 * GROUPS, 2 * g + s + 1))
                    if s == 0:
                        wait(act, sc_mm, at(f, HEADS, 4 * g))
                    act.activation(qk[:, s, :], f_ps[:, s, 0:T], ACT.Copy).then_inc(qk_copied, 1)

            def v_copy(f):
                for t in range(3):
                    act.wait_ge(v_mm, at(f, 3, t + 1))
                    if t == 0:
                        wait(act, av_mm, at(f, GROUPS, 0))
                    act.activation(v_s[:, t, :], f_ps[0:QT, 2 + t, 0:C + HD], ACT.Copy,
                                   scale=v_mask[:, t:t + 1]).then_inc(v_copied, 1)

            def softmax_exp(f, hd):
                act.wait_ge(nmx_done, at(f, HEADS, hd + 1))
                wait(act, pt_mm, at(f, 3 * HEADS, 3 * hd - 3))
                for t in range(3):
                    e = act.activation(prob[hd % 2][:, t, :], f_ps[0:QT, t, 0:T], ACT.Exp, scale=HD ** -0.5,
                                       bias=neg_max[:, hd % 2, t:t + 1], accum_out=row_sum[:, hd % 2, t:t + 1])
                e.then_inc(pexp, 1)

            def turn_copy(f, hd, lo, hi):
                if hd % 4 == 0 and lo == 0:
                    wait(act, av_mm, at(f, GROUPS, hd // 4))
                for t in range(lo, hi):
                    n = 3 * hd + t
                    act.wait_ge(pt_mm, at(f, 3 * HEADS, n + 1))
                    new = min(t, 1)
                    act.activation(prob_t[:, hd % 4, :, QS[t] + new:QS[t] + QT],
                                   f_ps[0:QT, 3 + n % 2, 0:3 * QT].rearrange("p (k t) -> p k t", k=3)[:, :, new:],
                                   ACT.Copy).then_inc(pt_copied, 1)

            def av_copy(f, g):
                act.wait_ge(av_mm, at(f, GROUPS, g + 1))
                if g == 0:
                    wait(act, pr_mm, at(f, 1, 0))
                act.activation(o_s[:, g, :], f_ps[:, 3, 0:T], ACT.Copy).then_inc(av_copied, 1)

            def fc1_copy(f, small, variants):
                for q in range(HC * variants[0], HC * (variants[-1] + 1)):
                    act.wait_ge(fc1_mm, mlp_at(f, small, q + 1))
                    act.activation(hid[:, q, :], f_ps[:, q % 2, 0:T], ACT.Identity,
                                   bias=fc1_b_s[:, q % HC:q % HC + 1]).then_inc(fc1_copied, 1)

            def gelus(f, small):
                for v in range(3 if small else 1):
                    act.wait_ge(fc1_copied, mlp_at(f, small, HC * (v + 1)))
                    part = hid[:, HC * v:HC * (v + 1), :]
                    act.activation(part, part, ACT.Gelu).then_inc(gelu_done, 1)
                act.preload_act_table_set("natural_log_exp_and_others")

            def fine_mid(f, small, gap):
                if gap in VAR_GAPS:
                    j = VAR_GAPS.index(gap)
                    rstd(f_ps[0:CH, 3, 0:T], rstd_f, f_var, at(f, 4, j + 1), f_ln, at(f, 4, j + 1), f_rstd)
                if gap in QK_GAPS:
                    qk_copy(f, QK_GAPS.index(gap))
                if gap == 13:
                    v_copy(f)
                if gap in TURN_GAPS:
                    turn_copy(f, TURN_GAPS.index(gap), 0, 2)
                if gap in AV_GAPS:
                    av_copy(f, AV_GAPS.index(gap))

            def fine_late(f, small, gap):
                if gap in (6, 8, 10, 33):
                    j = (6, 8, 10, 33).index(gap)
                    squares(cen[:, :, :] if j != 1 else res[:, :, :], sq_f, f_cen, at(f, 4, j + 1), f_sq)
                if gap in SCORE_GAPS:
                    softmax_exp(f, SCORE_GAPS.index(gap))
                if gap in TURN_GAPS:
                    turn_copy(f, TURN_GAPS.index(gap), 2, 3)
                if gap == 35:
                    fc1_copy(f, small, (0,))
                if gap == 36 and small:
                    fc1_copy(f, small, (1, 2))
                if gap == 37:
                    gelus(f, small)

            def fronts(b, d, a, gap):
                x, xd = (b, 1) if d == 0 else (a, 0)
                if x is not None:
                    if gap in (4, 5, 6):
                        xz_copy(x, xd, 2 * gap - 8, 2 * gap - 6)
                    if gap == 7:
                        silu(x, xd)
                    if gap == 8:
                        xproj_copy(x, xd)
                    if gap == 10:
                        dt_abs(x, xd, 0, 2)
                    if gap == 11:
                        dt_abs(x, xd, 2, 3)
                        softplus(x, xd)
                if d == 0 and a is not None and gap == 13:
                    rstd(a_ps[0:CH, 1, 0:T], rstd_a, a_var, at(a, 1, 1), a_ln, at(a, 1, 1), a_rstd)

            def fronts_late(b, d, a, gap):
                if d == 0 and a is not None and gap == 12:
                    squares(xn[parity(a)][:, :, :], sq_a, a_cen, at(a, 1, 1), a_sq)

            def step(b, f, e, a):
                for d in range(2):
                    for gap in range(GAPS):
                        q = d * 6 + gap // 3 + 1
                        lo, hi = [(0, 3), (3, 6), (6, 8)][gap % 3]
                        if q < SCANS:
                            exps(b, q, lo, hi)
                        elif a is not None:
                            exps(a, 0, lo, hi)
                        for part in endings(d, gap, f, e):
                            fine_mid(*part)
                        fronts(b, d, a, gap)
                        rows = bc_rows(b, d, a, gap)
                        if rows:
                            bc_copy(*rows)
                        fronts_late(b, d, a, gap)
                        for part in endings(d, gap, f, e):
                            fine_late(*part)

            def front():
                act.wait_ge(s_w, 16 * len(LOADS))
                act.wait_ge(s_cp, 8)
                act.wait_ge(s_c, CONSTS)
                act.preload_act_table_set("natural_log_exp_and_others")
                act.activation(inner_s[:, :, :, I_A:I_A + N], inner_s[:, :, :, I_A:I_A + N], ACT.Exp).then_inc(s_ca, 1)
                b = (0, 0)
                squares(xn[0][:, :, :], sq_a, a_cen, 1, a_sq)
                rstd(a_ps[0:CH, 1, 0:T], rstd_a, a_var, 1, a_ln, 1, a_rstd)
                xz_copy(b, 0, 0, 6)
                silu(b, 0)
                xproj_copy(b, 0)
                dt_abs(b, 0, 0, IC)
                softplus(b, 0)
                bc_copy(b, 0, 0, 32)
                act.wait_ge(a_neg, 1)
                exps(b, 0, 0, NH)

            def finish(f, e):
                for gap in range(2 * GAPS + 5):
                    if gap <= 4:
                        fine_mid(*e, 2 * GAPS + gap)
                        fine_late(*e, 2 * GAPS + gap)
                    fine_mid(*f, gap)
                    fine_late(*f, gap)

            program(step, act.Fori, front, finish)

        @block.vector
        def _(dve):
            def scan_step(b, q, phase):
                d, u, half = q // 6, (q // 2) % IC, q % 2
                x, dec = hs[half], decay[half]
                if phase == 0:
                    dve.wait_ge(dtu_ready, at(b, 2, d + 1))
                    dve.wait_ge(bc_copied, at(b, 64, 32 * d + 16 * half + 8))
                    wait(dve, ysum, at(b, SCANS, q - 1))
                    dve.tensor_tensor(x[:, :, :], states[half][:, :, :],
                                      dtu[d][:, u, :].unsqueeze(1).broadcast_to([128, NH, T]),
                                      ALU.mult).then_inc(dbu_done, 1)
                    if u == 0:
                        wait(dve, scan_done, at(b, SCANS, q - 1))
                        t = 0 if d == 0 else T - 1
                        dve.memset(dec[:, :, t:t + 1], 0.0).then_inc(edge, 1)
                if phase == 1:
                    dve.wait_ge(exp_done, at(b, SCANS, q + 1))
                    dve.wait_ge(dbu_done, at(b, SCANS, q + 1))
                    if u == 0:
                        dve.wait_ge(edge, at(b, 4, 2 * d + half + 1))
                    a = dec[:, :, :].rearrange("p n t -> p (n t)")
                    i = x[:, :, :].rearrange("p n t -> p (n t)")
                    if d == 1:
                        a, i = a[:, ::-1], i[:, ::-1]
                    dve.tensor_tensor_scan(i, a, i, 0.0, ALU.mult, ALU.add).then_inc(scan_done, 1)
                if phase == 2:
                    dve.wait_ge(scan_done, at(b, SCANS, q + 1))
                    dve.wait_ge(bc_copied, at(b, 64, 32 * d + 16 * half + 16))
                    dve.tensor_tensor(x[:, :, :], x[:, :, :], reads[half][:, :, :], ALU.mult).then_inc(hc_done, 1)

            def gate_unit(b, u):
                d, j = u // IC, u % IC
                dve.wait_ge(ysum, at(b, SCANS, 2 * u + 2))
                if u == 0:
                    wait(dve, out_mm, at(b, 1, 0))
                dve.scalar_tensor_tensor(out=yg[:, u, :], in0=xc[d][:, j, :], scalar=inner_s[:, d, j, I_D:I_D + 1],
                                         in1=y_ps[:, 0:T], op0=ALU.mult, op1=ALU.add).then_inc(gate_tmp, 1)
                dve.wait_ge(gate_tmp, at(b, UNITS, u + 1))
                dve.tensor_tensor(yg[:, u, :], yg[:, u, :], zs[d][:, j, :], ALU.mult).then_inc(gated, 1)

            def centre(x, out, bank, ready, value, done):
                dve.wait_ge(ready, value)
                dve.tensor_tensor(out[:, :, :], x[:, :, :], bank.unsqueeze(1).broadcast_to([CH, 2, T]),
                                  ALU.subtract).then_inc(done, 1)

            def scale_by(x, r, ready, value, done):
                dve.wait_ge(ready, value)
                dve.tensor_tensor(x[:, :, :], x[:, :, :], r[:, :].unsqueeze(1).broadcast_to([CH, 2, T]),
                                  ALU.mult).then_inc(done, 1)

            def affine(f, j, small):
                g = (P_N1LG, P_N1SG, P_N2LG, P_N2SG)[2 * j + small]
                dve.wait_ge(f_y, at(f, 4, 3 + j))
                for i in range(2):
                    a = dve.tensor_scalar(cen[:, i, :], cen[:, i, :], feat_s[:, i, g:g + 1],
                                          feat_s[:, i, g + 1:g + 2], ALU.mult, ALU.add)
                a.then_inc(f_aff, 1)

            def tok_add(b):
                dve.wait_ge(tok_mm, at(b, 1, 1))
                dve.scalar_tensor_tensor(
                    out=h[parity(b)][:, :, 1:1 + PATCHES],
                    in0=a_ps[0:CH, 0, 0:2 * PATCHES].rearrange("p (a t) -> p a t", a=2), scalar=1.0 / 255.0,
                    in1=feat_s[:, :, P_POS + 1:P_POS + 1 + PATCHES], op0=ALU.mult, op1=ALU.add)\
                    .then_inc(h_ready, 1)

            def conv(b, d, js):
                for k in range(TAPS):
                    for j in js:
                        before = TAPS * js[0] + len(js) * (k - 1) + j - js[0]
                        t = k if d == 0 else 2 * PAD - k
                        w = inner_s[:, d, j, k:k + 1]
                        if k == 0:
                            dve.wait_ge(xz_copied, at(b, 12, 6 * d + j + 1))
                            dve.tensor_scalar(xc[d][:, j, :], xi[:, j, t:t + T], w, inner_s[:, d, j, I_CB:I_CB + 1],
                                              ALU.mult, ALU.add).then_inc(conv_tap, 1)
                        else:
                            dve.wait_ge(conv_tap, at(b, 24, 12 * d + before + 1))
                            dve.scalar_tensor_tensor(out=xc[d][:, j, :], in0=xi[:, j, t:t + T], scalar=w,
                                                     in1=xc[d][:, j, :], op0=ALU.mult, op1=ALU.add)\
                                .then_inc(conv_tap, 1)

            def split_parts(b, d):
                dve.wait_ge(xp_hi, at(b, 2, d + 1))
                rest = dt[d][:, 0, :]
                dve.tensor_tensor(rest[64:128, :], a_ps[64:128, 0, 0:T], parts[64:128, :], ALU.subtract)\
                    .then_inc(split, 1)
                dve.wait_ge(split, at(b, 6, 3 * d + 1))
                dve.tensor_copy(parts[64:128, :], rest[64:128, :]).then_inc(split, 1)
                dve.wait_ge(split, at(b, 6, 3 * d + 2))
                dve.tensor_tensor(parts[96:128, :], rest[96:128, :], parts[96:128, :], ALU.subtract)\
                    .then_inc(split, 1)

            def dt_max(b, d, lo, hi):
                for j in range(lo, hi):
                    dve.wait_ge(dtv_abs, at(b, 6, 3 * d + j + 1))
                    if j == 0:
                        dve.wait_ge(split, at(b, 6, 3 * d + 3))
                    dve.tensor_scalar(dt[d][:, j, :], a_ps[:, (j + 1) % 2, 0:T], 0.0, None, ALU.max)\
                        .then_inc(dtv_max, 1)

            def dt_sum(b, d):
                dve.wait_ge(sp_ln, at(b, 2, d + 1))
                dve.wait_ge(dtv_max, at(b, 6, 3 * d + 3))
                dve.tensor_tensor(dt[d][:, :, :], dt[d][:, :, :], dtu[d][:, :, :], ALU.add).then_inc(dt_ready, 2)
                dve.wait_ge(dt_ready, at(b, 4, 2 * d + 2))
                dve.wait_ge(silu_done, at(b, 4, 2 * d + 2))
                dve.tensor_tensor(dtu[d][:, :, :], dt[d][:, :, :], xc[d][:, :, :], ALU.mult).then_inc(dtu_ready, 1)

            def residual(f):
                dve.wait_ge(out_mm, at(f, 1, 1))
                wait(dve, out_ready, at(f, 1, 0))
                dve.tensor_tensor(res[:, :, :], f_ps[0:CH, 3:5, 0:T], xn[parity(f)][:, :, :], ALU.add)\
                    .then_inc(r_ready, 1)

            def add_mixer(f):
                dve.wait_ge(f_y, at(f, 4, 1))
                wait(dve, out_stored, at(f, 16, 0))
                for i in range(2):
                    dve.scalar_tensor_tensor(out=h2[:, i, :], in0=cen[:, i, :],
                                             scalar=feat_s[:, i, P_LNG:P_LNG + 1], in1=h[parity(f)][:, i, :],
                                             op0=ALU.mult, op1=ALU.add).then_inc(h2_tmp, 1)
                dve.wait_ge(h2_tmp, at(f, 2, 2))
                for i in range(2):
                    a = dve.tensor_scalar(h2[:, i, :], h2[:, i, :], feat_s[:, i, P_LNB:P_LNB + 1], None, ALU.add)
                a.then_inc(h2_ready, 1)

            def row_maxima(f, hd):
                s = hd % 2
                dve.wait_ge(sc_mm, at(f, HEADS, hd + 1))
                dve.tensor_reduce(row_max[:, s, :], f_ps[0:QT, 0:3, 0:T], AX_X, ALU.max).then_inc(mx_done, 1)
                dve.wait_ge(mx_done, at(f, HEADS, hd + 1))
                dve.tensor_scalar(neg_max[:, s, :], row_max[:, s, :], -HD ** -0.5, None, ALU.mult)\
                    .then_inc(nmx_done, 1)

            def normalise(f, hd):
                s = hd % 2
                dve.wait_ge(pexp, at(f, HEADS, hd + 1))
                dve.reciprocal(row_inv[:, s, :], row_sum[:, s, :]).then_inc(inv_done, 1)
                dve.wait_ge(inv_done, at(f, HEADS, hd + 1))
                for t in range(3):
                    a = dve.tensor_scalar(prob[s][:, t, :], prob[s][:, t, :], row_inv[:, s, t:t + 1], None, ALU.mult)
                a.then_inc(p_norm, 1)

            def add_gated(banks, halves, g, added, by=1):
                dve.scalar_tensor_tensor(out=res[:, halves, :], in0=f_ps[0:CH, banks, 0:T], scalar=gate[:, g:g + 1],
                                         in1=res[:, halves, :], op0=ALU.mult, op1=ALU.add).then_inc(added, by)

            def add_biased(bank, i, p, added):
                dve.scalar_tensor_tensor(out=res[:, i, :], in0=f_ps[0:CH, bank, 0:T], scalar=feat_s[:, i, p:p + 1],
                                         in1=res[:, i, :], op0=ALU.add, op1=ALU.add).then_inc(added, 1)

            def add_bias_sum(i, j, added):
                dve.tensor_scalar(res[:, i, :], res[:, i, :], bias_sum[:, i, j:j + 1], None, ALU.add)\
                    .then_inc(added, 1)

            def add_attention(f, small):
                dve.wait_ge(pr_mm, at(f, 1, 1))
                start = uneven(f, small, 2, 5, 0)
                if small:
                    add_gated(slice(0, 2), slice(0, 2), 0, x3_step)
                    dve.wait_ge(x3_step, start + 1)
                    add_gated(2, 0, 1, x3_step)
                    dve.wait_ge(x3_step, start + 2)
                    add_gated(3, 0, 2, x3_step)
                    add_bias_sum(1, 0, x3_step)
                    dve.wait_ge(x3_step, start + 4)
                    add_bias_sum(0, 0, x3_step)
                else:
                    for i in range(2):
                        add_biased(i, i, P_BPROJ, x3_step)

            def add_mlp(f, small):
                dve.wait_ge(fc2_mm, variant_at(f, small, 1))
                if small:
                    add_gated(slice(3, 5), slice(0, 2), 0, mlp_added, 2)
                else:
                    for i in range(2):
                        add_biased(3 + i, i, P_BFC2, mlp_added)

            def last_sum(f, small):
                start = uneven(f, small, 0, 4, 0)
                dve.wait_ge(mlp_added, at(f, 2, 2))
                if small:
                    dve.wait_ge(fc2_mm, variant_at(f, True, 2))
                    add_gated(2, 0, 1, fin_step)
                    dve.wait_ge(fc2_mm, variant_at(f, True, 3))
                    dve.wait_ge(fin_step, start + 1)
                    add_gated(0, 0, 2, fin_step)
                    add_bias_sum(1, 1, fin_step)
                    dve.wait_ge(fin_step, start + 3)
                    add_bias_sum(0, 1, fin_step)
                    dve.wait_ge(fin_step, start + 4)
                dve.tensor_tensor(h2[:, :, :], h2[:, :, :], res[:, :, :], ALU.add).then_inc(out_ready, 1)

            def fine(f, small, gap):
                if gap == 5:
                    residual(f)
                if gap in (6, 8, 10, 33):
                    j = (6, 8, 10, 33).index(gap)
                    centre((res, h2, res, res)[j], (cen, res, cen, cen)[j], f_ps[0:CH, 2, 0:T],
                           f_mean, at(f, 4, j + 1), f_cen)
                if gap in VAR_GAPS:
                    j = VAR_GAPS.index(gap)
                    scale_by((cen, res, cen, cen)[j], rstd_f, f_rstd, at(f, 4, j + 1), f_y)
                    if j == 0:
                        add_mixer(f)
                    if j >= 2:
                        affine(f, j - 2, small)
                if gap in SCORE_GAPS:
                    row_maxima(f, SCORE_GAPS.index(gap))
                if gap - 1 in SCORE_GAPS:
                    normalise(f, SCORE_GAPS.index(gap - 1))
                if gap == 32:
                    add_attention(f, small)
                if gap == 38:
                    add_mlp(f, small)
                if gap == 39:
                    last_sum(f, small)

            def fronts(b, d, a, gap):
                x, xd = (b, 1) if d == 0 else (a, 0)
                if x is not None:
                    if gap == 5:
                        conv(x, xd, (0, 1))
                    if gap == 6:
                        conv(x, xd, (2,))
                    if gap == 8:
                        split_parts(x, xd)
                    if gap == 10:
                        dt_max(x, xd, 0, 2)
                    if gap == 11:
                        dt_max(x, xd, 2, 3)
                    if gap == 12:
                        dt_sum(x, xd)
                if d == 0 and a is not None:
                    if gap == 11:
                        tok_add(a)
                    if gap == 12:
                        centre(h[parity(a)], xn[parity(a)], a_ps[0:CH, 1, 0:T], a_mean, at(a, 1, 1), a_cen)
                    if gap == 13:
                        scale_by(xn[parity(a)], rstd_a, a_rstd, at(a, 1, 1), xn_ready)

            def step(b, f, e, a):
                for d in range(2):
                    for gap in range(GAPS):
                        q = d * 6 + gap // 3
                        if gap % 6 == 3:
                            if q // 2 >= 1:
                                gate_unit(b, q // 2 - 1)
                            elif not first(b):
                                gate_unit(ago(b, 1), UNITS - 1)
                        scan_step(b, q, gap % 3)
                        for part in endings(d, gap, f, e):
                            fine(*part)
                        fronts(b, d, a, gap)

            def front():
                dve.memset(mean_w[:, :], 1.0 / C).then_inc(s_c, 1)
                dve.memset(eps_c[:, :], EPS).then_inc(s_c, 1)
                dve.memset(one_c[:, :], 1.0).then_inc(s_c, 1)
                dve.memset(xi[:, :, :], 0.0).then_inc(s_c, 1)
                dve.memset(dt_lo[:, :], 1.0).then_inc(s_c, 1)
                dve.wait_ge(s_w, 16 * len(LOADS))
                for i in range(2):
                    for c in range(2):
                        dve.tensor_tensor(h[c][:, i, 0:1], feat_s[:, i, P_CLS:P_CLS + 1],
                                          feat_s[:, i, P_POS:P_POS + 1], ALU.add).then_inc(s_c, 1)
                    dve.tensor_scalar(feat_s[:, i, P_POS + 1:FEAT_W], feat_s[:, i, P_POS + 1:FEAT_W],
                                      feat_s[:, i, P_TOKB:P_TOKB + 1], None, ALU.add).then_inc(s_c, 1)
                dve.memset(gate[2 * C // 6:CH, 2:3], 0.0).then_inc(s_c, 1)
                dve.wait_ge(s_c, 12)
                dve.tensor_reduce(gate_sum[:, 0:1], gate[:, 0:3], AX_X, ALU.add).then_inc(s_c, 1)
                dve.tensor_copy(gate_sum[:, 1:2], gate[:, 0:1]).then_inc(s_c, 1)
                dve.wait_ge(s_c, 14)
                for i in range(2):
                    for j, p in enumerate((P_BPROJ, P_BFC2)):
                        dve.tensor_tensor(bias_sum[:, i, j:j + 1], feat_s[:, i, p:p + 1], gate_sum[:, i:i + 1],
                                          ALU.mult).then_inc(s_c, 1)
                dve.wait_ge(s_c, CONSTS)
                b = (0, 0)
                tok_add(b)
                centre(h[0], xn[0], a_ps[0:CH, 1, 0:T], a_mean, 1, a_cen)
                dve.wait_ge(s_ca, 1)
                dve.tensor_scalar(inner_s[:, :, :, I_A:I_A + N], inner_s[:, :, :, I_A:I_A + N], -1.0, None,
                                  ALU.mult).then_inc(a_neg, 1)
                scale_by(xn[0], rstd_a, a_rstd, 1, xn_ready)
                conv(b, 0, (0, 1, 2))
                split_parts(b, 0)
                dt_max(b, 0, 0, IC)
                dt_sum(b, 0)

            def finish(f, e):
                for gap in range(2 * GAPS + 5):
                    if gap == 3:
                        gate_unit(f[0], UNITS - 1)
                    if gap <= 4:
                        fine(*e, 2 * GAPS + gap)
                    fine(*f, gap)

            program(step, dve.Fori, front, finish)


def kernel(**inputs):
    import numpy as np
    import concourse.bacc as bacc
    from concourse.bass_utils import run_bass_kernel_spmd as run

    a = {k: np.asarray(v) for k, v in inputs.items()}

    def halves(w):
        return w.reshape(2, CH, *w.shape[1:]).swapaxes(0, 1)

    def chunks(w):
        return w.reshape(-1, 128, *w.shape[1:]).swapaxes(0, 1)

    def both(f):
        return np.stack([f("L0_attn_f_"), f("L0_attn_b_")], axis=1)

    def x_proj(p):
        w = a[p + "xp"].T
        wide = np.zeros((INNER, 128), w.dtype)
        wide[:, :RANK] = w[:, :RANK]
        for q in (32, 64, 96):
            wide[:, q:q + 2 * N] = w[:, RANK:]
        return chunks(wide)

    def inner(p):
        return chunks(np.concatenate([a[p + "cw"].T, a[p + "cb"][:, None], a[p + "D"][:, None], a[p + "Alog"]], 1))

    def spaced(w):
        wide = np.zeros((*w.shape[:-1], HEADS, 2 * HD), w.dtype)
        wide[..., :HD] = w.reshape(*w.shape[:-1], HEADS, HD)
        return wide.reshape(*w.shape[:-1], HEADS * 2 * HD)

    ff = "L0_ffn_"
    x = a["x"].reshape(BATCH, 14, 16, 14, 48).transpose(0, 2, 4, 1, 3)
    w_qkv = a[ff + "w_qkv"]
    vectors = [a["L0_tok_b"], a["L0_tok_class_token"], a["L0_attn_ln_g"], a["L0_attn_ln_b"]]
    vectors += [a[ff + n] for n in ("n1l_g", "n1l_b", "n1s_g", "n1s_b", "n2l_g", "n2l_b", "n2s_g", "n2s_b",
                                    "b_proj", "b_fc2")]
    arrays = {
        "patches": x.reshape(BATCH, KP, 128, PATCHES).transpose(0, 2, 1, 3),
        "txt": a["txt"].transpose(0, 2, 1).reshape(BATCH, 2, CH, TXT).transpose(0, 2, 1, 3),
        "tok_w": chunks(a["L0_tok_W"]),
        "feat": halves(np.concatenate([np.stack(vectors, 1), a["L0_tok_pos_emb"].T], 1)),
        "w_in": halves(both(lambda p: a[p + "in"].T)),
        "inner": both(inner),
        "x_proj": both(x_proj),
        "dt_w": both(lambda p: np.concatenate([a[p + "dtw"].T, a[p + "dtb"][None]], 0)),
        "w_out": both(lambda p: chunks(a[p + "out"].T)),
        "w_qk": halves(np.stack([spaced(w_qkv[:, :C]), spaced(w_qkv[:, C:2 * C])], 1)),
        "w_v": halves(np.pad(w_qkv[:, 2 * C:], ((0, 0), (0, HD)))),
        "w_proj": chunks(spaced(a[ff + "w_proj"].T).T),
        "fc1": halves(a[ff + "w_fc1"]),
        "fc1_b": chunks(a[ff + "b_fc1"]),
        "fc2": chunks(a[ff + "w_fc2"]),
        "gumbel": np.broadcast_to(a[ff + "gumbel_weights"], (CH, 3)),
    }
    arrays = {k: np.ascontiguousarray(v) for k, v in arrays.items()}
    nc = bacc.Bacc("TRN2", target_bir_lowering=False, num_devices=1)
    args = {k: nc.dram_tensor(f"in_{k}", v.shape, mybir.dt.from_np(v.dtype), kind="ExternalInput").ap()
            for k, v in arrays.items()}
    out = nc.dram_tensor("out_0", (BATCH, CH, 2, T), F32, kind="ExternalOutput").ap()
    build(nc, **args, out=out)
    r = run(nc, [{f"in_{k}": v for k, v in arrays.items()}], core_ids=[0])
    got = r.results[0]["out_0"]
    return np.ascontiguousarray(got.transpose(0, 3, 2, 1).reshape(BATCH, T, C))
```
